# Optimizing a Trainium2 kernel written in Bass

```python
import numpy as np
import jax
import jax.numpy as jnp

def _softmax(x, axis=-1):
    return jax.nn.softmax(x, axis=axis)

def _gelu(x):
    return jax.nn.gelu(x, approximate=True)

def _silu(x):
    return jax.nn.silu(x)

def _sigmoid(x):
    return jax.nn.sigmoid(x)

def _layernorm(x, axis=-1, eps=1e-05):
    m = jnp.mean(x, axis=axis, keepdims=True)
    v = jnp.var(x, axis=axis, keepdims=True)
    return (x - m) / jnp.sqrt(v + eps)

def _scatter_add(tgt, idx, src, axis=0):
    return tgt.at[idx].add(src)

def _segment_sum(src, seg, n):
    return jax.ops.segment_sum(src, seg, n)
kernel_name = 'mk_early_fusion_d1_tok_img1024_r4_4831ce'

def setup_inputs(seed: int=0):
    np.random.seed(seed)
    _w = jnp.asarray

    def _rec_inputs():
        import jax
        import jax.numpy as jnp
        _rk = jax.random.key(seed)
        x = -0.00016672 + 0.999947 * jax.random.normal(jax.random.fold_in(_rk, 1), (16, 3, 96, 96), jnp.float32)
        txt = 0.434251 + 1.14597 * jax.random.normal(jax.random.fold_in(_rk, 2), (16, 32, 256), jnp.float32)
        return (x, txt)
    x, txt = _rec_inputs()

    def _L0_tok_setup():
        import jax, jax.numpy as jnp
        import numpy as np
        DIM = 256
        IMG = 96
        P = 16
        C = 3
        TEMP = 10000.0
        EPS = 1e-05
        PATCH_DIM = C * P * P
        HP = IMG // P

        def layernorm(x, gamma, beta):
            mu = jnp.mean(x, axis=-1, keepdims=True)
            var = jnp.var(x, axis=-1, keepdims=True)
            return (x - mu) * jax.lax.rsqrt(var + EPS) * gamma + beta

        def posemb_sincos_2d(h, w, dim, dtype):
            y, x = jnp.meshgrid(jnp.arange(h), jnp.arange(w), indexing='ij')
            omega = jnp.arange(dim // 4, dtype=jnp.float32) / (dim // 4 - 1)
            omega = 1.0 / TEMP ** omega
            y = y.reshape(-1)[:, None] * omega[None, :]
            x = x.reshape(-1)[:, None] * omega[None, :]
            pe = jnp.concatenate((jnp.sin(x), jnp.cos(x), jnp.sin(y), jnp.cos(y)), axis=1)
            return pe.astype(dtype)
        key = jax.random.key(seed)
        ks = jax.random.split(key, 8)
        B = 64
        img = jax.random.normal(ks[0], (B, C, IMG, IMG), dtype=jnp.float32)
        cls_token = jax.random.normal(ks[1], (1, 1, DIM), dtype=jnp.float32)
        cls_pos_embedding = jax.random.normal(ks[2], (1, 1, DIM), dtype=jnp.float32)
        ln1_g = jnp.ones((PATCH_DIM,), jnp.float32)
        ln1_b = jnp.zeros((PATCH_DIM,), jnp.float32)
        W = jax.random.normal(ks[3], (PATCH_DIM, DIM), dtype=jnp.float32) / np.sqrt(PATCH_DIM)
        bias = jnp.zeros((DIM,), jnp.float32)
        ln2_g = jnp.ones((DIM,), jnp.float32)
        ln2_b = jnp.zeros((DIM,), jnp.float32)
        return {'img': img, 'cls_token': cls_token, 'cls_pos_embedding': cls_pos_embedding, 'ln1_g': ln1_g, 'ln1_b': ln1_b, 'W': W, 'bias': bias, 'ln2_g': ln2_g, 'ln2_b': ln2_b}
    _L0_tok_all = _L0_tok_setup()
    _L0_tok_in = {k: v for k, v in _L0_tok_all.items() if k in ('cls_token', 'cls_pos_embedding', 'ln1_g', 'ln1_b', 'W', 'bias', 'ln2_g', 'ln2_b')}
    del _L0_tok_all

    def _L0_attn_setup():
        import jax, jax.numpy as jnp
        import numpy as np
        B, M, D = (8, 512, 256)

        def _rope_tables(m, d):
            i = jnp.arange(d // 2, dtype=jnp.float32)
            theta = jnp.power(jnp.float32(10000.0), -2.0 * (i - 1.0) / d)
            ang = jnp.arange(m, dtype=jnp.float32)[:, None] * theta[None, :]
            return (jnp.cos(ang), jnp.sin(ang))

        def _rotate(t, cos, sin):
            te, to = (t[..., 0::2], t[..., 1::2])
            re = te * cos + to * sin
            ro = -te * sin + to * cos
            return jnp.stack([re, ro], axis=-1).reshape(t.shape)
        key = jax.random.key(seed)
        kx, kq, kk, kv = jax.random.split(key, 4)
        x = jax.random.normal(kx, (B, M, D), dtype=jnp.float32)
        wq = jax.random.normal(kq, (D, D), dtype=jnp.float32) * 0.02
        wk = jax.random.normal(kk, (D, D), dtype=jnp.float32) * 0.02
        wv = jax.random.normal(kv, (D, D), dtype=jnp.float32) * 0.02
        return {'x': x, 'wq': wq, 'wk': wk, 'wv': wv}
    _L0_attn_all = _L0_attn_setup()
    _L0_attn_in = {k: v for k, v in _L0_attn_all.items() if k in ('wq', 'wk', 'wv')}
    del _L0_attn_all

    def _L0_ffn_setup():
        import jax, jax.numpy as jnp
        import numpy as np
        H, F, E_SHARED, E_ROUTED, K = (256, 1024, 1, 8, 2)

        def _expert(x, w_up, w_down):
            h = jax.nn.gelu(jnp.einsum('bsh,hf->bsf', x, w_up), approximate=False)
            return jnp.einsum('bsf,fh->bsh', h, w_down)
        key = jax.random.key(seed)
        ks = jax.random.split(key, 6)
        x = jax.random.normal(ks[0], (4, 512, H), dtype=jnp.float32)
        s = 0.02
        shared_up = jax.random.normal(ks[1], (E_SHARED, H, F), dtype=jnp.float32) * s
        shared_down = jax.random.normal(ks[2], (E_SHARED, F, H), dtype=jnp.float32) * s
        routed_up = jax.random.normal(ks[3], (E_ROUTED, H, F), dtype=jnp.float32) * s
        routed_down = jax.random.normal(ks[4], (E_ROUTED, F, H), dtype=jnp.float32) * s
        router_w = jax.random.normal(ks[5], (H, E_ROUTED), dtype=jnp.float32) * s
        return {'x': x, 'shared_up': shared_up, 'shared_down': shared_down, 'routed_up': routed_up, 'routed_down': routed_down, 'router_w': router_w}
    _L0_ffn_all = _L0_ffn_setup()
    _L0_ffn_in = {k: v for k, v in _L0_ffn_all.items() if k in ('shared_up', 'shared_down', 'routed_up', 'routed_down', 'router_w')}
    del _L0_ffn_all
    return {'x': x, 'txt': txt, 'L0_tok_cls_token': _L0_tok_in['cls_token'], 'L0_tok_cls_pos_embedding': _L0_tok_in['cls_pos_embedding'], 'L0_tok_ln1_g': _L0_tok_in['ln1_g'], 'L0_tok_ln1_b': _L0_tok_in['ln1_b'], 'L0_tok_W': _L0_tok_in['W'], 'L0_tok_bias': _L0_tok_in['bias'], 'L0_tok_ln2_g': _L0_tok_in['ln2_g'], 'L0_tok_ln2_b': _L0_tok_in['ln2_b'], 'L0_attn_wq': _L0_attn_in['wq'], 'L0_attn_wk': _L0_attn_in['wk'], 'L0_attn_wv': _L0_attn_in['wv'], 'L0_ffn_shared_up': _L0_ffn_in['shared_up'], 'L0_ffn_shared_down': _L0_ffn_in['shared_down'], 'L0_ffn_routed_up': _L0_ffn_in['routed_up'], 'L0_ffn_routed_down': _L0_ffn_in['routed_down'], 'L0_ffn_router_w': _L0_ffn_in['router_w']}

def reference(x, txt, L0_tok_cls_token, L0_tok_cls_pos_embedding, L0_tok_ln1_g, L0_tok_ln1_b, L0_tok_W, L0_tok_bias, L0_tok_ln2_g, L0_tok_ln2_b, L0_attn_wq, L0_attn_wk, L0_attn_wv, L0_ffn_shared_up, L0_ffn_shared_down, L0_ffn_routed_up, L0_ffn_routed_down, L0_ffn_router_w):
    import jax
    import jax.numpy as jnp

    def _L0_tok_ref(img, cls_token, cls_pos_embedding, ln1_g, ln1_b, W, bias, ln2_g, ln2_b):
        import jax, jax.numpy as jnp
        import numpy as np
        DIM = 256
        IMG = 96
        P = 16
        C = 3
        TEMP = 10000.0
        EPS = 1e-05
        PATCH_DIM = C * P * P
        HP = IMG // P

        def layernorm(x, gamma, beta):
            mu = jnp.mean(x, axis=-1, keepdims=True)
            var = jnp.var(x, axis=-1, keepdims=True)
            return (x - mu) * jax.lax.rsqrt(var + EPS) * gamma + beta

        def posemb_sincos_2d(h, w, dim, dtype):
            y, x = jnp.meshgrid(jnp.arange(h), jnp.arange(w), indexing='ij')
            omega = jnp.arange(dim // 4, dtype=jnp.float32) / (dim // 4 - 1)
            omega = 1.0 / TEMP ** omega
            y = y.reshape(-1)[:, None] * omega[None, :]
            x = x.reshape(-1)[:, None] * omega[None, :]
            pe = jnp.concatenate((jnp.sin(x), jnp.cos(x), jnp.sin(y), jnp.cos(y)), axis=1)
            return pe.astype(dtype)
        b = img.shape[0]
        x = img.reshape(b, C, HP, P, HP, P)
        x = jnp.transpose(x, (0, 2, 4, 3, 5, 1))
        x = x.reshape(b, HP, HP, PATCH_DIM)
        x = layernorm(x, ln1_g, ln1_b)
        x = jnp.einsum('bhwp,pd->bhwd', x, W) + bias
        x = layernorm(x, ln2_g, ln2_b)
        pe = posemb_sincos_2d(HP, HP, DIM, x.dtype)
        x = x.reshape(b, HP * HP, DIM) + pe[None]
        cls_tokens = jnp.broadcast_to(cls_token + cls_pos_embedding, (b, 1, DIM))
        return jnp.concatenate((cls_tokens, x), axis=1)

    def _L0_attn_ref(x, wq, wk, wv):
        import jax, jax.numpy as jnp
        import numpy as np
        B, M, D = (8, 512, 256)

        def _rope_tables(m, d):
            i = jnp.arange(d // 2, dtype=jnp.float32)
            theta = jnp.power(jnp.float32(10000.0), -2.0 * (i - 1.0) / d)
            ang = jnp.arange(m, dtype=jnp.float32)[:, None] * theta[None, :]
            return (jnp.cos(ang), jnp.sin(ang))

        def _rotate(t, cos, sin):
            te, to = (t[..., 0::2], t[..., 1::2])
            re = te * cos + to * sin
            ro = -te * sin + to * cos
            return jnp.stack([re, ro], axis=-1).reshape(t.shape)
        b, m, d = x.shape
        q = x @ wq.T
        k = x @ wk.T
        v = x @ wv.T
        cos, sin = _rope_tables(m, d)
        qr = _rotate(q, cos, sin)
        kr = _rotate(k, cos, sin)
        scale = 1.0 / jnp.sqrt(jnp.float32(d))
        scores = jnp.einsum('bqd,bkd->bqk', qr, kr) * scale
        attn = jax.nn.softmax(scores, axis=-1)
        return jnp.einsum('bqk,bkd->bqd', attn, v)

    def _L0_ffn_ref(x, shared_up, shared_down, routed_up, routed_down, router_w):
        import jax, jax.numpy as jnp
        import numpy as np
        H, F, E_SHARED, E_ROUTED, K = (256, 1024, 1, 8, 2)

        def _expert(x, w_up, w_down):
            h = jax.nn.gelu(jnp.einsum('bsh,hf->bsf', x, w_up), approximate=False)
            return jnp.einsum('bsf,fh->bsh', h, w_down)
        shared_out = jnp.zeros_like(x)
        for i in range(E_SHARED):
            shared_out = shared_out + _expert(x, shared_up[i], shared_down[i])
        probs = jax.nn.softmax(jnp.einsum('bsh,he->bse', x, router_w), axis=-1)
        top_k_prob, top_k_idx = jax.lax.top_k(probs, K)
        onehot = jax.nn.one_hot(top_k_idx, E_ROUTED, dtype=x.dtype)
        gates = jnp.einsum('bsk,bske->bse', top_k_prob, onehot)
        routed_out = jnp.zeros_like(x)
        for e in range(E_ROUTED):
            y = _expert(x, routed_up[e], routed_down[e])
            routed_out = routed_out + gates[..., e:e + 1] * y
        return shared_out + routed_out + x
    h = _L0_tok_ref(x, L0_tok_cls_token, L0_tok_cls_pos_embedding, L0_tok_ln1_g, L0_tok_ln1_b, L0_tok_W, L0_tok_bias, L0_tok_ln2_g, L0_tok_ln2_b)
    h = jnp.concatenate([h, txt], axis=1)
    h = h + _L0_attn_ref(_layernorm(h, axis=-1), L0_attn_wq, L0_attn_wk, L0_attn_wv)
    h = h + _L0_ffn_ref(_layernorm(h, axis=-1), L0_ffn_shared_up, L0_ffn_shared_down, L0_ffn_routed_up, L0_ffn_routed_down, L0_ffn_router_w)
    return h

_drawn_inputs = setup_inputs


def setup_inputs(seed=0):
    import zlib

    import numpy as np

    out = dict(_drawn_inputs(seed))
    spreads = {'L0_tok_ln1_g': (1.0, 0.2),
     'L0_tok_ln1_b': (0.0, 0.1),
     'L0_tok_bias': (0.0, 0.1),
     'L0_tok_ln2_g': (1.0, 0.2),
     'L0_tok_ln2_b': (0.0, 0.1)}
    factors = {'L0_attn_wq': 8.0,
     'L0_attn_wk': 8.0,
     'L0_ffn_routed_up': 4.599,
     'L0_ffn_routed_down': 4.481,
     'L0_ffn_router_w': 5.043}
    for name, (base, spread) in spreads.items():
        noise = np.random.default_rng([zlib.crc32(name.encode()), seed]).standard_normal(out[name].shape)
        drawn = base * np.exp(spread * noise) if base else spread * noise
        out[name] = jnp.asarray(drawn.astype(out[name].dtype))
    for name, factor in factors.items():
        out[name] = (out[name] * factor).astype(out[name].dtype)
    return out
```

```python
from contextlib import ExitStack

import concourse.bass as bass
from concourse import mybir

F32 = mybir.dt.float32
F32R = mybir.dt.float32r
I32 = mybir.dt.int32
U32 = mybir.dt.uint32
ALU = mybir.AluOpType
ACT = mybir.ActivationFunctionType
AX = mybir.AxisListType

P = 128
NB, NPATCH, NTXT, D, F, NE = 16, 36, 32, 256, 1024, 8
SEQ = 1 + NPATCH + NTXT
T = NB * SEQ
PATCH = 768
EPS = 1e-5
KD = D // P
KF = F // P
TOK = 96
NTOK = NB * NPATCH // TOK
KP = PATCH // P
GB = 4
NG = NB // GB
GT = GB * SEQ
QSCALE = 1.0 / 16.0
NT = -(-T // P)
TPAD = NT * P
ROWS = [min(P, T - P * i) for i in range(NT)]
SG = 3
NSG = NT // SG
SN = SG * P
TILES = (2 * T - NE) // P + NE
XW = D + 5
C_TOK2, C_EXP, C_GATE = D, D + 1, D + 3
CAP = -(-T // P)
RING = 3
EW = 2 * KD * F
UPW = KD * F
NX = NE + 1

S_VALID, S_RANK, S_THR, S_TILE = 0, NT, NT + NE, NT + NE + CAP
S_TOK2 = S_TILE + TILES
S_ONE = S_TOK2 + NT + 1
NSMALL = S_ONE + NE


def fusion_layer(nc, patches, txt, cls_token, cls_pos, ln1_gb, tok_w, tok_bias, ln2_g, ln2_b,
                 wq, wk, wv, w_up, w_dn, router_w, c_mats, c_small, c_pe, c_rope, out):
    ctx = ExitStack()
    early = ExitStack()
    shared = ExitStack()

    def sb(name, shape, dt=F32, where=ctx, side="left"):
        return where.enter_context(nc.sbuf_tensor(name, shape, dt, side=side))

    def sem(name):
        return ctx.enter_context(nc.semaphore(name))

    img_d = nc.dram_tensor("img_tokens", [NB * NPATCH, D], F32).ap()
    h2_d = nc.dram_tensor("h_after_attention", [T, D], F32).ap()
    slots_d = nc.dram_tensor("slots", [TILES * P, XW], F32).ap()
    z_d = nc.dram_tensor("gated_outputs", [2 * T, D], F32).ap()

    with ctx:
        mats = sb("mats", [P, 3, P])
        ident, upper, ones = mats[:, 0, :], mats[:, 1, :], mats[:, 2, :]
        small = sb("small", [P, NSMALL])
        half_neg = sb("half_neg", [P, NT])
        hx = sb("hx", [P, NT, XW])
        base = sb("base", [P, NT, D])
        stage = sb("stage", [P, 2, UPW])
        gact = sb("gact", [P, 2, SN])
        hT_n = sb("hT_n", [P, 2, KD, TPAD], F32R, shared, "right")
        hid = sb("hid", [P, 2, KF, SN], F32R, shared, "right")
        shared.close()
        rout = sb("rout", [P, 8, NT * NE])
        rsm = sb("rsm", [P, 8, NT])
        rtab = sb("rtab", [P, 4, NE])
        rpick = sb("rpick", [P, 2, NT * NE])
        rsel = sb("rsel", [P, (NT + 1) * NE])
        rcmp = sb("rcmp", [P, NE * CAP])
        etab = sb("etab", [P, TILES])
        ecmp = sb("ecmp", [P, TILES * NE])
        e_int = sb("e_int", [1, TILES], I32)
        ering = sb("ering", [1, TILES], I32)
        ekeep = sb("ekeep", [1, 2, TILES])
        tend_int = sb("tend_int", [1, NE], I32)
        slot_i = sb("slot_i", [P, 2, NT], I32)
        rw = sb("rw", [P, KD, NE])
        rws = sb("rws", [P, 2, KD, NE], F32R)
        st2 = sb("st2", [P, 6])
        mv2 = sb("mv2", [P, NT, 2])
        rs2 = sb("rs2", [P, NT])
        h2f = sb("h2f", [P, 2, D])
        ring0_pad = early.enter_context(nc.sbuf_tensor("ring0_pad", [P, 2 * EW], F32))

        xp = sb("xp", [TOK, NTOK, PATCH], where=early)
        tw = sb("tw", [P, KP, D], where=early)
        lngb = sb("lngb", [P, 2, KP], where=early)
        xT = sb("xT", [P, 2, KP, TOK], where=early)
        tt = sb("tt", [TOK, 2, D], where=early)
        pe = sb("pe", [TOK, NTOK, D], where=early)
        vecs = sb("vecs", [TOK, 3, D], where=early)
        tst = sb("tst", [TOK, NTOK, 12], where=early)
        tmv = sb("tmv", [TOK, 2 * NTOK, 2], where=early)
        trs = sb("trs", [TOK, 2 * NTOK], where=early)
        clsr = sb("clsr", [1, 3, D], where=early)
        wqk = sb("wqk", [P, 2, KD, D], where=early)
        wvs = sb("wvs", [P, KD, D], where=early)
        rope = sb("rope", [P, 2, SEQ], where=early)
        h = sb("h", [SEQ, 2, GB, D], where=early)
        hn = sb("hn", [SEQ, GB, D], where=early)
        ast = sb("ast", [SEQ, GB, 6], where=early)
        amv = sb("amv", [SEQ, GB, 2], where=early)
        ars = sb("ars", [SEQ, GB], where=early)
        hT = sb("hT", [P, KD, GT], where=early)
        rtmp = sb("rtmp", [P, 2, 2, GT], where=early)
        qk = sb("qk", [P, 2, 2, GT], where=early)
        vv = sb("vv", [SEQ, 2, GB, D], where=early)
        sc = sb("sc", [SEQ, GB, SEQ], where=early)
        pr = sb("pr", [SEQ, GB, SEQ], where=early)
        asm = sb("asm", [SEQ, 3, GB], where=early)
        prT = sb("prT", [SEQ, GB, SEQ], where=early)
        early.close()

        ring = sb("ring", [P, RING, 2, EW], F32R)
        xg = sb("xg", [P, 2, XW])
        xgT = sb("xgT", [P, 2, 2, KD, P], F32R)
        hg = sb("hg", [P, 2, F])
        hgT = sb("hgT", [P, 2, 2, KF, P], F32R, side="right")
        gate = sb("gate", [P, TILES])
        junk = sb("junk", [P, 2, 2])
        dest = sb("dest", [P, TILES], I32)
        y_all = sb("y_all", [P, TILES, D], side="right")
        hx_flat = hx[:, :, :].rearrange("p n w -> p (n w)")
        zt = hx_flat[:, 0:6 * D].rearrange("p (n w) -> p n w", n=3)
        fin = hx_flat[:, 6 * D:9 * D].rearrange("p (n w) -> p n w", n=3)

        ps = ctx.enter_context(nc.psum_tensor("ps", [P, 8, 512], F32))

        patches_in = [sem(f"patches_in{i}") for i in range(NTOK)]
        tok_w_in, tok_vec_in, consts_in = sem("tok_w_in"), sem("tok_vec_in"), sem("consts_in")
        attn_w_in, cls_in, router_in = sem("attn_w_in"), sem("cls_in"), sem("router_in")
        exps_in = sem("exps_in")
        s_dve = sem("dve_chain")
        s_pool = sem("pool_chain")
        t_stats, t_rstd = sem("t_stats"), sem("t_rstd")
        t_normed, t_tr, t_affA, t_affV = sem("t_normed"), sem("t_tr"), sem("t_affA"), sem("t_affV")
        t_mm, t_stats2, t_rstd2, t_done = sem("t_mm"), sem("t_stats2"), sem("t_rstd2"), sem("t_done")
        pe_ready, cls_ready = sem("pe_ready"), sem("cls_ready")
        img_out = [sem(f"img_out{i}") for i in range(NTOK)]
        h_in = [sem(f"h_in{i}") for i in range(2)]
        a_stats, a_rstd, a_normed, a_tr, a_hT = (sem(n) for n in ("a_stats", "a_rstd", "a_normed", "a_tr", "a_hT"))
        a_qk, a_rope, a_v, a_vs = (sem(n) for n in ("a_qk", "a_rope", "a_v", "a_vs"))
        a_scores, a_sub, a_exp, a_pT, a_pTs = (sem(n) for n in ("a_scores", "a_sub", "a_exp", "a_pT", "a_pTs"))
        a_pv, a_h2, h2_out = sem("a_pv"), sem("a_h2"), sem("h2_out")
        f_in = [sem(f"f_in{i}") for i in range(2)]
        f_stats, f_rstd, f_normed, f_base, f_tr, f_hi, f_lo = (
            sem(n) for n in ("f_stats", "f_rstd", "f_normed", "f_base", "f_tr", "f_hi", "f_lo"))
        pads, rws_ready, logits = sem("pads"), sem("rws_ready"), sem("logits")
        r_sub, r_exp, r_mask, r_prefix, r_slots, r_tiles = (
            sem(n) for n in ("r_sub", "r_exp", "r_mask", "r_prefix", "r_slots", "r_tiles"))
        slot_free = sem("slot_free")
        empty_row = sem("empty_row")
        slots_init, slots_out = sem("slots_init"), sem("slots_out")
        w_in = [sem(f"w_in{i}") for i in range(2)]
        w_free, w_ready = sem("w_free"), sem("w_ready")
        s_up, s_act, s_hi, s_lo, s_down, s_base = (
            sem(n) for n in ("s_up", "s_act", "s_hi", "s_lo", "s_down", "s_base"))
        x_in = [sem(f"x_in{i}") for i in range(2)]
        x_tr, x_meta, x_hi, x_lo = sem("x_tr"), sem("x_meta"), sem("x_hi"), sem("x_lo")
        e_up, e_act, e_tr, e_hi, e_lo = (sem(n) for n in ("e_up", "e_act", "e_tr", "e_hi", "e_lo"))
        ffn_done, y_ready, z_out = sem("ffn_done"), sem("y_ready"), sem("z_out")
        z_in = [sem(f"z_in{i}") for i in range(3)]
        o_ready, o_out = sem("o_ready"), sem("o_out")

        needs = [-(-(P * i + ROWS[i]) // GT) for i in range(NT)]

        def flat_tiles_after(g):
            return [i for i in range(NT) if needs[i] == g]

        block = ctx.enter_context(nc.Block())

        def run_steps(eng, step):
            for s in range(-2, 3):
                step(s, s % 2, first=True, up=s >= -1, tr=s >= 0)
            pairs = (TILES - 2 - 3) // 2
            with eng.Fori(0, pairs) as i:
                for c in range(2):
                    step(2 * i + (3 + c), (3 + c) % 2)
            for s in range(3 + 2 * pairs, TILES + 1):
                step(s, s % 2, x=s + 2 < TILES, up=s + 1 < TILES, tr=s < TILES)

        @block.sync
        def _(sp):
            for i in range(NTOK):
                sp.dma_start(xp[:, i, :], patches[TOK * i:TOK * (i + 1), :]).then_inc(patches_in[i], 16)

            sp.wait_ge(empty_row, 1)
            sp.dma_start(slots_d.rearrange("(t p) w -> p t w", p=P),
                         gact[:, 0:1, 0:XW].to_broadcast([P, TILES, XW])).then_inc(slots_init, 16)

            def store_group(g):
                sp.wait_ge(a_h2, g + 1)
                sp.dma_start(h2_d[GT * g:GT * (g + 1), :].rearrange("(b s) d -> s b d", s=SEQ),
                             h[:, g % 2, :, :]).then_inc(h2_out, 16)
                sp.wait_ge(h2_out, 16 * (g + 1))
                for i in flat_tiles_after(g + 1):
                    if i >= 2:
                        sp.wait_ge(f_base, i - 1)
                    sp.dma_start(h2f[0:ROWS[i], i % 2, :], h2_d[P * i:P * i + ROWS[i], :]).then_inc(f_in[i % 2], 16)

            for i in range(NTOK):
                sp.wait_ge(t_done, i + 1)
                sp.dma_start(img_d[TOK * i:TOK * (i + 1), :], tt[:, i % 2, :]).then_inc(img_out[i], 16)
            sp.wait_ge(cls_ready, 1)
            for g in range(NG):
                for i in range(NTOK):
                    if TOK * i < NPATCH * GB * (g + 1):
                        sp.wait_ge(img_out[i], 16)
                sp.dma_start(h[0:1, g % 2, :, :], clsr[0:1, 2:3, :].to_broadcast([1, GB, D])).then_inc(h_in[g % 2], 16)
                sp.dma_start(h[1:1 + NPATCH, g % 2, :, :],
                             img_d[NPATCH * GB * g:NPATCH * GB * (g + 1), :].rearrange("(b s) d -> s b d", s=NPATCH)
                             ).then_inc(h_in[g % 2], 16)
                sp.dma_start(h[1 + NPATCH:SEQ, g % 2, :, :],
                             txt[GB * g:GB * (g + 1), :, :].rearrange("b s d -> s b d")).then_inc(h_in[g % 2], 16)
                if g >= 1:
                    store_group(g - 1)
            store_group(NG - 1)

            sp.wait_ge(slots_out, 16 * 2 * NT)
            for t in range(2):
                sp.dma_start(xg[:, t, :], slots_d[P * t:P * (t + 1), :]).then_inc(x_in[t], 16)
            with sp.Fori(0, (TILES - 3) // 2) as i:
                for c in range(2):
                    sp.wait_ge(x_tr, 2 * i + (1 + c))
                    sp.wait_ge(x_meta, 2 * i + (1 + c))
                    sp.dma_start(xg[:, c, :], slots_d[bass.ds(2 * P * i + P * (2 + c), P), :]).then_inc(x_in[c], 16)
            t = TILES - 1
            sp.wait_ge(x_tr, t - 1)
            sp.wait_ge(x_meta, t - 1)
            sp.dma_start(xg[:, t % 2, :], slots_d[P * t:P * (t + 1), :]).then_inc(x_in[t % 2], 16)

            sp.wait_ge(z_out, 16 * TILES)
            for i in range(NT + 2):
                if i < NT:
                    if i >= 3:
                        sp.wait_ge(o_ready, i - 2)
                    sp.dma_start(zt[0:ROWS[i], i % 3, :],
                                 z_d[2 * P * i:2 * P * i + 2 * ROWS[i], :].rearrange("(p k) d -> p (k d)", k=2)
                                 ).then_inc(z_in[i % 3], 16)
                if i >= 2:
                    sp.wait_ge(o_ready, i - 1)
                    sp.dma_start(out[P * (i - 2):P * (i - 2) + ROWS[i - 2], :],
                                 fin[0:ROWS[i - 2], (i - 2) % 3, :]).then_inc(o_out, 16)
                    sp.wait_ge(o_out, 16 * (i - 1))

        @block.gpsimd
        def _(pool):
            link_count = [0]

            def link(ins):
                link_count[0] += 1
                ins.then_inc(s_pool, 1)
                pool.wait_ge(s_pool, link_count[0])

            def load_weights(n):
                if n < 2 * NX:
                    if n >= 2:
                        pool.wait_ge(w_free, n - 1)
                    pool.dma_start(stage[:, n % 2, :], (w_up, w_dn)[n % 2][n // 2, :, :]).then_inc(w_in[n % 2], 16)

            def tiles_before(x):
                return pool.value_load(tend_int[0:1, x - 1:x], min_val=0, max_val=TILES)

            def split_weights(x, part):
                load_weights(2 * x + part + 1)
                if x >= RING and part == 0:
                    if x == RING:
                        pool.wait_ge(ffn_done, 1)
                    else:
                        pool.wait_ge(ffn_done, tiles_before(x - RING) + 1)
                    pool.sem_inc(slot_free, 1)
                pool.wait_ge(w_in[part], 16 * (x + 1))
                cols = slice(part * UPW, (part + 1) * UPW)
                hi, lo = ring[:, x % RING, 0, cols], ring[:, x % RING, 1, cols]
                link(nc.gpsimd.tensor_scalar(hi, stage[:, part, :], 1.0, 0.0, ALU.mult, ALU.add))
                low = nc.gpsimd.tensor_tensor(lo, stage[:, part, :], hi.bitcast(F32), ALU.subtract)
                low.then_inc(w_free, 1)
                if part == 1:
                    pool.wait_ge(w_free, 2 * x + 2)
                    pool.sem_inc(w_ready, 1)

            def prepare(x):
                for part in range(2):
                    split_weights(x, part)

            link(nc.gpsimd.memset(half_neg[:, :], -0.5))
            nc.gpsimd.memset(hT_n[:, :, :, T:TPAD].bitcast(F32), 0.0).then_inc(pads, 1)
            pool.wait_ge(tok_vec_in, 16 * 4)
            for i in range(NTOK):
                last = nc.gpsimd.tensor_tensor(pe[:, i, :], pe[:, i, :], vecs[:, 2, :], ALU.add)
            last.then_inc(pe_ready, 1)
            pool.wait_ge(cls_in, 32)
            nc.gpsimd.tensor_tensor(clsr[:, 2, :], clsr[:, 0, :], clsr[:, 1, :], ALU.add).then_inc(cls_ready, 1)
            pool.wait_ge(t_stats, 1)
            nc.gpsimd.tensor_tensor(trs[:, 0:NTOK], tmv[:, 0:NTOK, 1], half_neg[0:TOK, 0:NTOK], ALU.pow).then_inc(t_rstd, 1)
            for i in range(NTOK):
                pool.wait_ge(t_stats2, i + 1)
                nc.gpsimd.tensor_tensor(trs[:, NTOK + i:NTOK + i + 1], tmv[:, NTOK + i, 1:2], half_neg[0:TOK, 0:1],
                                        ALU.pow).then_inc(t_rstd2, 1)
            load_weights(0)

            def flat_roots(g):
                for i in flat_tiles_after(g):
                    pool.wait_ge(f_stats, i + 1)
                    nc.gpsimd.tensor_tensor(rs2[0:ROWS[i], i:i + 1], mv2[0:ROWS[i], i, 1:2], half_neg[0:ROWS[i], 0:1],
                                            ALU.pow).then_inc(f_rstd, 1)

            for g in range(NG):
                pool.wait_ge(a_stats, g + 1)
                nc.gpsimd.tensor_tensor(ars[:, :], amv[:, :, 1], half_neg[0:SEQ, 0:GB], ALU.pow).then_inc(a_rstd, 1)
                if g < 2:
                    split_weights(0, g)
                if g >= 1:
                    flat_roots(g)
            flat_roots(NG)

            pool.wait_ge(a_h2, NG)
            pool.wait_ge(h2_out, 16 * NG)
            prepare(1)
            pool.wait_ge(slots_init, 16)
            pool.wait_ge(r_slots, 1)
            for i in range(NT):
                for k in range(2):
                    pool.indirect_dma_start(
                        slots_d, bass.IndirectOffsetOnAxis(ap=slot_i[0:ROWS[i], k, i:i + 1].bitcast(U32), axis=0),
                        hx[0:ROWS[i], i, :], None).then_inc(slots_out, 16)
            prepare(2)
            for x in range(RING, NX):
                prepare(x)
            for t in range(TILES):
                pool.wait_ge(y_ready, t + 1)
                pool.indirect_dma_start(z_d, bass.IndirectOffsetOnAxis(ap=dest[:, t:t + 1].bitcast(U32), axis=0),
                                        y_all[:, t, :], None, bounds_check=2 * T - 1, oob_is_err=False
                                        ).then_inc(z_out, 16)

        @block.scalar
        def _(act):
            act.dma_start(mats[:, :, :], c_mats).then_inc(consts_in, 16)
            act.dma_start(small[:, :], c_small).then_inc(consts_in, 16)
            act.dma_start(lngb[:, :, :], ln1_gb).then_inc(consts_in, 16)
            act.dma_start(tw[:, :, :], tok_w.rearrange("(k p) d -> p k d", p=P)).then_inc(tok_w_in, 16)
            act.dma_start(pe[:, :, :], c_pe).then_inc(tok_vec_in, 16)
            for n, v in enumerate((tok_bias, ln2_g, ln2_b)):
                act.dma_start(vecs[:, n, :], v.partition_broadcast(TOK)).then_inc(tok_vec_in, 16)
            act.dma_start(clsr[:, 0, :], cls_token).then_inc(cls_in, 16)
            act.dma_start(clsr[:, 1, :], cls_pos).then_inc(cls_in, 16)
            act.dma_start(wqk[:, 0, :, :], wq.rearrange("(k p) d -> p k d", p=P)).then_inc(attn_w_in, 16)
            act.dma_start(wqk[:, 1, :, :], wk.rearrange("(k p) d -> p k d", p=P)).then_inc(attn_w_in, 16)
            act.dma_start(wvs[:, :, :], wv.rearrange("(k p) d -> p k d", p=P)).then_inc(attn_w_in, 16)
            act.dma_start(rope[:, :, :], c_rope).then_inc(attn_w_in, 16)
            act.dma_start(rw[:, :, :], router_w.rearrange("(k p) e -> p k e", p=P)).then_inc(router_in, 16)

            act.wait_ge(consts_in, 48)
            for i in range(NTOK):
                act.wait_ge(t_tr, i + 1)
                if i >= 2:
                    act.wait_ge(t_mm, i - 1)
                for c in range(KP // 2):
                    last = nc.scalar.activation(xT[:, i % 2, c, :], ps[:, 2 * (i % 2), TOK * c:TOK * (c + 1)],
                                                ACT.Identity, bias=lngb[:, 1, c:c + 1], scale=lngb[:, 0, c:c + 1])
                last.then_inc(t_affA, 1)

            def flat_high(g):
                for i in flat_tiles_after(g):
                    act.wait_ge(f_tr, i + 1)
                    nc.scalar.activation(hT_n[:, 0, :, P * i:P * i + ROWS[i]],
                                         ps[:, i % 2, 0:KD * P].rearrange("p (k t) -> p k t", k=KD)[:, :, 0:ROWS[i]],
                                         ACT.Copy).then_inc(f_hi, 1)

            for g in range(NG):
                act.wait_ge(a_tr, g + 1)
                if g >= 1:
                    act.wait_ge(a_v, g)
                nc.scalar.activation(hT[:, :, :], ps[:, 0:2, 0:GT], ACT.Copy).then_inc(a_hT, 1)
                act.wait_ge(a_v, g + 1)
                if g >= 2:
                    act.wait_ge(a_pv, g - 1)
                nc.scalar.activation(vv[:, g % 2, :, :].rearrange("p (a b) d -> p a (b d)", a=2),
                                     ps[0:SEQ, 0:2, :], ACT.Copy).then_inc(a_vs, 1)
                act.wait_ge(a_sub, g + 1)
                if g >= 1:
                    act.wait_ge(a_pT, g)
                nc.scalar.activation(pr[:, :, :], sc[:, :, :], ACT.Exp, scale=QSCALE).then_inc(a_exp, 1)
            for g in range(1, NG + 1):
                flat_high(g)
            act.wait_ge(r_sub, 1)
            nc.scalar.activation(rout[:, 1, :], rout[:, 0, :], ACT.Exp).then_inc(r_exp, 1)

            act.wait_ge(slots_init, 16)
            for n in range(NSG * KF):
                act.wait_ge(s_up, n + 1)
                if n >= 2:
                    act.wait_ge(s_lo, n - 1)
                nc.scalar.activation(gact[:, n % 2, :], ps[:, 2 + n % 4, 0:SN], ACT.Gelu).then_inc(s_act, 1)

            def step(s, c, first=False, x=True, up=True, tr=True):
                if x:
                    act.wait_ge(x_tr, s + 3)
                    if not (first and s < 0):
                        act.wait_ge(e_up, 2 * s + 2)
                    nc.scalar.activation(xgT[:, c, 0, :, :], ps[:, 4, 0:KD * P].rearrange("p (k t) -> p k t", k=KD),
                                         ACT.Copy).then_inc(x_hi, 1)
                if up:
                    if not (first and s < 1):
                        act.wait_ge(e_tr, 2 * s)
                    for half in range(2):
                        act.wait_ge(e_up, 2 * s + (3 + half))
                        nc.scalar.activation(hg[:, 1 - c, 512 * half:512 * (half + 1)], ps[:, half, :],
                                             ACT.Gelu).then_inc(e_act, 1)
                if tr:
                    if not (first and s < 2):
                        act.wait_ge(ffn_done, s)
                    for half in range(2):
                        act.wait_ge(e_tr, 2 * s + (1 + half))
                        nc.scalar.activation(hgT[:, c, 0, 4 * half:4 * half + 4, :],
                                             ps[:, 2 + half, :].rearrange("p (k t) -> p k t", k=4),
                                             ACT.Copy).then_inc(e_hi, 1)

            run_steps(act, step)

        @block.tensor
        def _(te):
            def transpose(o, i, n):
                return nc.tensor.transpose(o, i, ident[0:n, 0:n])

            te.wait_ge(consts_in, 48)
            te.wait_ge(tok_w_in, 16)

            def tok_transposes(i):
                te.wait_ge(t_normed, i + 1)
                if i >= 2:
                    te.wait_ge(t_affA, i - 1)
                    te.wait_ge(t_affV, i - 1)
                for c in range(KP):
                    last = transpose(ps[:, 2 * (i % 2) + c // 3, TOK * (c % 3):TOK * (c % 3 + 1)],
                                     xp[:, i, P * c:P * (c + 1)], TOK)
                last.then_inc(t_tr, 1)

            def tok_product(i):
                te.wait_ge(t_affA, i + 1)
                te.wait_ge(t_affV, i + 1)
                if i >= 2:
                    te.wait_ge(t_stats2, i - 1)
                for c in range(KP):
                    last = nc.tensor.matmul(ps[0:TOK, 4 + i % 2, 0:D], xT[:, i % 2, c, :], tw[:, c, :],
                                            start=c == 0, stop=c == KP - 1)
                last.then_inc(t_mm, 1)

            tok_transposes(0)
            for i in range(NTOK):
                if i + 1 < NTOK:
                    tok_transposes(i + 1)
                tok_product(i)

            te.wait_ge(attn_w_in, 64)
            te.wait_ge(t_stats2, NTOK)

            def attention_back(g):
                te.wait_ge(a_exp, g + 1)
                if g >= 1:
                    te.wait_ge(a_h2, g)
                for b in range(GB):
                    last = transpose(ps[0:SEQ, 6, SEQ * b:SEQ * (b + 1)], pr[:, b, :], SEQ)
                last.then_inc(a_pT, 1)
                te.wait_ge(a_pTs, g + 1)
                te.wait_ge(a_vs, g + 1)
                for b in range(GB):
                    last = nc.tensor.matmul(ps[0:SEQ, (7, 6)[b // 2], D * (b % 2):D * (b % 2 + 1)], prT[:, b, :],
                                            vv[:, g % 2, b, :], start=True, stop=True)
                last.then_inc(a_pv, 1)

            for g in range(NG):
                te.wait_ge(a_normed, g + 1)
                if g >= 1:
                    te.wait_ge(a_vs, g)
                for b in range(GB):
                    for c in range(KD):
                        last = transpose(ps[:, c, SEQ * b:SEQ * (b + 1)], hn[:, b, P * c:P * (c + 1)], SEQ)
                last.then_inc(a_tr, 1)
                te.wait_ge(a_hT, g + 1)
                if g >= 1:
                    te.wait_ge(a_rope, g)
                for eo in range(2):
                    for w in range(2):
                        for c in range(KD):
                            last = nc.tensor.matmul(ps[:, 2 + 2 * eo + w, 0:GT], wqk[:, w, c, P * eo:P * (eo + 1)],
                                                    hT[:, c, :], start=c == 0, stop=c == KD - 1)
                last.then_inc(a_qk, 1)
                for b in range(GB):
                    for c in range(KD):
                        last = nc.tensor.matmul(ps[0:SEQ, b // 2, D * (b % 2):D * (b % 2 + 1)],
                                                hT[:, c, SEQ * b:SEQ * (b + 1)], wvs[:, c, :],
                                                start=c == 0, stop=c == KD - 1)
                last.then_inc(a_v, 1)
                if g >= 1:
                    attention_back(g - 1)
                te.wait_ge(a_rope, g + 1)
                if g >= 1:
                    te.wait_ge(a_h2, g)
                for b in range(GB):
                    for c in range(KD):
                        last = nc.tensor.matmul(ps[0:SEQ, 7, SEQ * b:SEQ * (b + 1)], qk[:, c, 0, SEQ * b:SEQ * (b + 1)],
                                                qk[:, c, 1, SEQ * b:SEQ * (b + 1)], start=c == 0, stop=c == KD - 1)
                last.then_inc(a_scores, 1)
            attention_back(NG - 1)

            te.wait_ge(rws_ready, 1)
            te.wait_ge(pads, 1)
            te.wait_ge(a_h2, NG)

            def flat_transposes(i):
                te.wait_ge(f_normed, i + 1)
                if i >= 2:
                    te.wait_ge(f_lo, i - 1)
                for c in range(KD):
                    last = transpose(ps[:, i % 2, P * c:P * c + ROWS[i]], hx[0:ROWS[i], i, P * c:P * (c + 1)], ROWS[i])
                last.then_inc(f_tr, 1)

            def split_product(o, pairs):
                for n, (a, b) in enumerate(pairs):
                    nc.tensor.matmul(o, a[0], b[0], start=n == 0, stop=False)
                    nc.tensor.matmul(o, a[0], b[1], start=False, stop=False)
                    last = nc.tensor.matmul(o, a[1], b[0], start=False, stop=n == len(pairs) - 1)
                return last

            flat_transposes(0)
            for i in range(NT):
                if i + 1 < NT:
                    flat_transposes(i + 1)
                te.wait_ge(f_lo, i + 1)
                last = split_product(ps[:, 7, NE * i:NE * (i + 1)],
                                     [([hT_n[:, v, c, P * i:P * (i + 1)] for v in range(2)],
                                       [rws[:, v, c, :] for v in range(2)]) for c in range(KD)])
            last.then_inc(logits, 1)

            def shared_up(q):
                for f in range(KF):
                    n = KF * q + f
                    if n >= 4:
                        te.wait_ge(s_act, n - 3)
                    split_product(ps[:, 2 + n % 4, 0:SN],
                                  [([ring[:, 0, v, F * c + P * f:F * c + P * (f + 1)] for v in range(2)],
                                    [hT_n[:, v, c, SN * q:SN * (q + 1)] for v in range(2)]) for c in range(KD)]
                                  ).then_inc(s_up, 1)

            def shared_down(q):
                te.wait_ge(s_lo, KF * (q + 1))
                for j in range(SG):
                    i = SG * q + j
                    if i >= 2:
                        te.wait_ge(s_base, i - 1)
                    split_product(ps[:, i % 2, 0:D],
                                  [([hid[:, v, f, P * j:P * (j + 1)] for v in range(2)],
                                    [ring[:, 0, v, UPW + D * f:UPW + D * (f + 1)] for v in range(2)])
                                   for f in range(KF)]).then_inc(s_down, 1)

            te.wait_ge(w_ready, 1)
            shared_up(0)
            te.wait_ge(r_mask, 1)
            nc.tensor.matmul(ps[:, 6, 0:NE * (NT + 1)], upper, rsel[:, :], start=True, stop=False)
            for i in range(NT):
                last = nc.tensor.matmul(ps[:, 6, NE * (i + 1):NE * (NT + 1)].rearrange("p (n e) -> p n e", e=NE), ones,
                                        rsel[:, NE * i:NE * (i + 1)].unsqueeze(1).to_broadcast([P, NT - i, NE]),
                                        start=False, stop=i == NT - 1)
            last.then_inc(r_prefix, 1)
            shared_down(0)
            for q in range(1, NSG):
                shared_up(q)
                shared_down(q)
            te.wait_ge(s_down, NT)
            te.sem_inc(ffn_done, 1)
            te.wait_ge(s_base, NT)
            te.wait_ge(r_tiles, 1)

            def step(s, c, first=False, x=True, up=True, tr=True):
                if x:
                    te.wait_ge(x_in[c], 8 * s + (32 - 8 * c))
                    if not (first and s < -1):
                        te.wait_ge(x_lo, s + 2)
                    for k in range(KD):
                        last = transpose(ps[:, 4, P * k:P * (k + 1)], xg[:, c, P * k:P * (k + 1)], P)
                    last.then_inc(x_tr, 1)
                if up:
                    te.wait_ge(x_lo, s + 2)
                    place = te.value_load(ering[0:1, bass.ds(s + 1, 1)], min_val=0, max_val=RING - 1)
                    count = te.value_load(e_int[0:1, bass.ds(s + 1, 1)], min_val=0, max_val=NE - 1)
                    te.wait_ge(w_ready, count + 2)
                    w = ring[:, bass.ds(place, 1), :, :].rearrange("p a v n -> p (a v) n")
                    for half in range(2):
                        if not (first and s < 0):
                            te.wait_ge(e_act, 2 * s + (1 + half))
                        split_product(ps[:, half, :],
                                      [([xgT[:, 1 - c, v, k, :] for v in range(2)],
                                        [w[:, v, F * k + 512 * half:F * k + 512 * (half + 1)] for v in range(2)])
                                       for k in range(KD)]).then_inc(e_up, 1)
                if tr:
                    for half in range(2):
                        te.wait_ge(e_act, 2 * s + (1 + half))
                        if not (first and s < 1):
                            te.wait_ge(e_lo, 2 * s + (half - 1))
                        for k in range(4):
                            f = 4 * half + k
                            last = transpose(ps[:, 2 + half, P * k:P * (k + 1)], hg[:, c, P * f:P * (f + 1)], P)
                        last.then_inc(e_tr, 1)
                if not (first and s < 1):
                    te.wait_ge(e_lo, 2 * s)
                    if not (first and s < 2):
                        te.wait_ge(y_ready, s - 1)
                    place = te.value_load(ering[0:1, bass.ds(s - 1, 1)], min_val=0, max_val=RING - 1)
                    w = ring[:, bass.ds(place, 1), :, :].rearrange("p a v n -> p (a v) n")
                    split_product(ps[:, 5, 0:D],
                                  [([hgT[:, 1 - c, v, k, :] for v in range(2)],
                                    [w[:, v, UPW + D * k:UPW + D * (k + 1)] for v in range(2)])
                                   for k in range(KF)]).then_inc(ffn_done, 1)

            run_steps(te, step)

        @block.vector
        def _(dve):
            v = nc.vector
            link_count = [0]

            def link(ins):
                link_count[0] += 1
                ins.then_inc(s_dve, 1)
                dve.wait_ge(s_dve, link_count[0])

            dve.wait_ge(consts_in, 48)
            link(v.memset(gact[:, 0, 0:XW], 0.0))
            v.memset(gact[:, 0, C_EXP:C_EXP + 2], -1.0)
            v.tensor_copy(gact[:, 0, C_TOK2:C_TOK2 + 1], small[:, S_TOK2 + NT:S_TOK2 + NT + 1]).then_inc(empty_row, 1)
            link(v.tensor_copy(hx[:, :, C_TOK2], small[:, S_TOK2:S_TOK2 + NT]))

            for i in range(NTOK):
                dve.wait_ge(patches_in[i], 16)
                for j in range(2):
                    last = v.bn_stats(tst[:, i, 6 * j:6 * j + 6], xp[:, i, 384 * j:384 * (j + 1)])
            link(last)
            for i in range(NTOK):
                last = v.bn_aggr(tmv[:, i, :], tst[:, i, :])
            link(last)
            v.tensor_scalar(tmv[:, 0:NTOK, 1], tmv[:, 0:NTOK, 1], EPS, None, ALU.add).then_inc(t_stats, 1)
            dve.wait_ge(t_rstd, 1)

            def tok_norm(i):
                v.tensor_scalar(xp[:, i, :], xp[:, i, :], tmv[:, i, 0:1], trs[:, i:i + 1], ALU.subtract,
                                ALU.mult).then_inc(t_normed, 1)

            def tok_affine(i):
                dve.wait_ge(t_tr, i + 1)
                if i >= 2:
                    dve.wait_ge(t_mm, i - 1)
                for c in range(KP // 2, KP):
                    last = v.tensor_scalar(xT[:, i % 2, c, :],
                                           ps[:, 2 * (i % 2) + 1, TOK * (c - 3):TOK * (c - 2)],
                                           lngb[:, 0, c:c + 1], lngb[:, 1, c:c + 1], ALU.mult, ALU.add)
                last.then_inc(t_affV, 1)

            def tok_stats(i):
                dve.wait_ge(t_mm, i + 1)
                if i >= 2:
                    dve.wait_ge(img_out[i - 2], 16)
                link(v.tensor_tensor(tt[:, i % 2, :], ps[0:TOK, 4 + i % 2, 0:D], vecs[:, 0, :], ALU.add))
                link(v.bn_stats(tst[:, i, 0:6], tt[:, i % 2, :]))
                link(v.bn_aggr(tmv[:, NTOK + i, :], tst[:, i, 0:6]))
                v.tensor_scalar(tmv[:, NTOK + i, 1:2], tmv[:, NTOK + i, 1:2], EPS, None, ALU.add).then_inc(t_stats2, 1)

            def tok_finish(i):
                dve.wait_ge(t_rstd2, i + 1)
                o = tt[:, i % 2, :]
                link(v.tensor_scalar(o, o, tmv[:, NTOK + i, 0:1], trs[:, NTOK + i:NTOK + i + 1], ALU.subtract, ALU.mult))
                link(v.tensor_tensor(o, o, vecs[:, 1, :], ALU.mult))
                v.tensor_tensor(o, o, pe[:, i, :], ALU.add).then_inc(t_done, 1)

            tok_norm(0)
            tok_norm(1)
            dve.wait_ge(tok_vec_in, 64)
            dve.wait_ge(pe_ready, 1)
            for i in range(NTOK):
                tok_affine(i)
                if i + 2 < NTOK:
                    tok_norm(i + 2)
                if i >= 1:
                    tok_finish(i - 1)
                tok_stats(i)
            tok_finish(NTOK - 1)

            dve.wait_ge(router_in, 16)
            link(v.tensor_copy(rws[:, 0, :, :], rw[:, :, :]))
            v.tensor_tensor(rws[:, 1, :, :], rw[:, :, :], rws[:, 0, :, :].bitcast(F32), ALU.subtract).then_inc(rws_ready, 1)

            cos, sin = (rope[:, n:n + 1, :].to_broadcast([P, GB, SEQ]) for n in range(2))

            def attention_front(g):
                u = g % 2
                dve.wait_ge(h_in[u], 48 * (g // 2 + 1))
                for b in range(GB):
                    last = v.bn_stats(ast[:, b, :], h[:, u, b, :])
                link(last)
                for b in range(GB):
                    last = v.bn_aggr(amv[:, b, :], ast[:, b, :])
                link(last)
                v.tensor_scalar(amv[:, :, 1], amv[:, :, 1], EPS, None, ALU.add).then_inc(a_stats, 1)
                dve.wait_ge(a_rstd, g + 1)
                if g >= 1:
                    dve.wait_ge(a_tr, g)
                for b in range(GB):
                    last = v.tensor_scalar(hn[:, b, :], h[:, u, b, :], amv[:, b, 0:1], ars[:, b:b + 1],
                                           ALU.subtract, ALU.mult)
                last.then_inc(a_normed, 1)

            def attention_rope(g):
                dve.wait_ge(a_qk, g + 1)
                if g >= 1:
                    dve.wait_ge(a_scores, g)
                for eo in range(2):
                    a, b = ((cos, sin), (sin, cos))[eo]
                    for n, tab in enumerate((a, b)):
                        for w in range(2):
                            last = v.tensor_tensor(
                                rtmp[:, n, w, :].rearrange("p (b s) -> p b s", b=GB),
                                ps[:, 2 + 2 * n + w, 0:GT].rearrange("p (b s) -> p b s", b=GB), tab, ALU.mult)
                    link(last)
                    if eo == 0:
                        link(v.tensor_tensor(qk[:, 0, :, :], rtmp[:, 0, :, :], rtmp[:, 1, :, :], ALU.add))
                    else:
                        v.tensor_tensor(qk[:, 1, :, :], rtmp[:, 1, :, :], rtmp[:, 0, :, :], ALU.subtract).then_inc(a_rope, 1)
                dve.wait_ge(a_rope, g + 1)

            def attention_softmax(g):
                dve.wait_ge(a_scores, g + 1)
                s3 = ps[0:SEQ, 7, 0:GT].rearrange("p (b s) -> p b s", b=GB)
                link(v.tensor_reduce(asm[:, 0, :], s3, AX.X, ALU.max))
                if g >= 1:
                    dve.wait_ge(a_exp, g)
                v.tensor_tensor(sc[:, :, :], s3, asm[:, 0, :].unsqueeze(2).to_broadcast([SEQ, GB, SEQ]),
                                ALU.subtract).then_inc(a_sub, 1)

            def attention_sums(g):
                dve.wait_ge(a_exp, g + 1)
                link(v.tensor_reduce(asm[:, 1, :], pr[:, :, :], AX.X, ALU.add))
                link(v.reciprocal(asm[:, 2, :], asm[:, 1, :]))
                dve.wait_ge(a_pT, g + 1)
                if g >= 1:
                    dve.wait_ge(a_pv, g)
                v.tensor_copy(prT[:, :, :], ps[0:SEQ, 6, 0:GT].rearrange("p (b s) -> p b s", b=GB)).then_inc(a_pTs, 1)

            def attention_end(g):
                dve.wait_ge(a_pv, g + 1)
                for b in range(GB):
                    last = v.scalar_tensor_tensor(
                        out=h[:, g % 2, b, :], in0=ps[0:SEQ, (7, 6)[b // 2], D * (b % 2):D * (b % 2 + 1)],
                        scalar=asm[:, 2, b:b + 1], in1=h[:, g % 2, b, :], op0=ALU.mult, op1=ALU.add)
                last.then_inc(a_h2, 1)

            def flat_tile(i):
                r = ROWS[i]
                dve.wait_ge(f_in[i % 2], 16 * (i // 2 + 1))
                x = h2f[0:r, i % 2, :]
                link(v.bn_stats(st2[0:r, :], x))
                link(v.bn_aggr(mv2[0:r, i, :], st2[0:r, :]))
                v.tensor_scalar(mv2[0:r, i, 1:2], mv2[0:r, i, 1:2], EPS, None, ALU.add).then_inc(f_stats, 1)
                dve.wait_ge(f_rstd, i + 1)
                v.tensor_scalar(hx[0:r, i, 0:D], x, mv2[0:r, i, 0:1], rs2[0:r, i:i + 1], ALU.subtract,
                                ALU.mult).then_inc(f_normed, 1)
                dve.wait_ge(f_normed, i + 1)
                v.tensor_tensor(base[0:r, i, :], x, hx[0:r, i, 0:D], ALU.add).then_inc(f_base, 1)

            def flat_low(i):
                r = ROWS[i]
                dve.wait_ge(f_hi, i + 1)
                cols = slice(P * i, P * i + r)
                v.tensor_tensor(hT_n[:, 1, :, cols], ps[:, i % 2, 0:KD * P].rearrange("p (k t) -> p k t", k=KD)[:, :, 0:r],
                                hT_n[:, 0, :, cols].bitcast(F32), ALU.subtract).then_inc(f_lo, 1)

            for g in range(NG + 1):
                if g < NG:
                    attention_front(g)
                if g >= 1:
                    attention_sums(g - 1)
                    attention_end(g - 1)
                if g < NG:
                    attention_rope(g)
                    attention_softmax(g)
                    if g >= 1:
                        for i in flat_tiles_after(g):
                            flat_tile(i)
            for i in flat_tiles_after(NG):
                flat_tile(i)
                if i == flat_tiles_after(NG)[0]:
                    for j in range(i):
                        flat_low(j)
            for j in flat_tiles_after(NG):
                flat_low(j)

            n3 = lambda a: a.rearrange("p (n e) -> p n e", e=NE)
            over_e = lambda a: a.unsqueeze(2).to_broadcast([P, NT, NE])
            rank = small[:, S_RANK:S_RANK + NE].unsqueeze(1).to_broadcast([P, NT, NE])
            dve.wait_ge(logits, 1)
            lg = n3(ps[:, 7, 0:NT * NE])
            link(v.tensor_reduce(rsm[:, 0, :], lg, AX.X, ALU.max))
            v.tensor_tensor(n3(rout[:, 0, :]), lg, over_e(rsm[:, 0, :]), ALU.subtract).then_inc(r_sub, 1)
            dve.wait_ge(r_exp, 1)
            link(v.tensor_reduce(rsm[:, 1, :], n3(rout[:, 1, :]), AX.X, ALU.add))
            link(v.reciprocal(rsm[:, 2, :], rsm[:, 1, :]))
            link(v.tensor_tensor(n3(rout[:, 2, :]), n3(rout[:, 1, :]), over_e(rsm[:, 2, :]), ALU.mult))
            for k in range(2):
                pk, gk = rout[:, 2 + k, :], rsm[:, 3 + k, :]
                pick = rpick[:, k, :]
                link(v.tensor_reduce(gk, n3(pk), AX.X, ALU.max))
                link(v.tensor_tensor(n3(rout[:, 4, :]), n3(pk), over_e(gk), ALU.is_equal))
                link(v.tensor_tensor(n3(rout[:, 4, :]), n3(rout[:, 4, :]), rank, ALU.mult))
                link(v.tensor_reduce(rsm[:, 5 + k, :], n3(rout[:, 4, :]), AX.X, ALU.max))
                link(v.tensor_tensor(n3(pick), over_e(rsm[:, 5 + k, :]), rank, ALU.is_equal))
                if k == 0:
                    link(v.scalar_tensor_tensor(out=rout[:, 3, :], in0=pick, scalar=-2.0, in1=pk,
                                                op0=ALU.mult, op1=ALU.add))
            link(v.tensor_tensor(rsel[:, 0:NE * NT], rpick[:, 0, :], rpick[:, 1, :], ALU.add))
            v.memset(rsel[:, NE * NT:], 0.0)
            link(v.tensor_tensor(n3(rsel[:, 0:NE * NT]), n3(rsel[:, 0:NE * NT]),
                                 over_e(small[:, S_VALID:S_VALID + NT]), ALU.mult))
            for k in range(2):
                v.tensor_copy(hx[:, :, C_GATE + k], rsm[:, 3 + k, :])
                last = v.tensor_scalar(hx[:, :, C_EXP + k], rsm[:, 5 + k, :], -1.0, float(NE), ALU.mult, ALU.add)
            last.then_inc(r_mask, 1)

            def shared_parts(q):
                for f in range(KF):
                    n = KF * q + f
                    dve.wait_ge(s_act, n + 1)
                    if f == 0 and q >= 1:
                        dve.wait_ge(s_down, SG * q)
                    link(v.tensor_copy(hid[:, 0, f, :], gact[:, n % 2, :]))
                    v.tensor_tensor(hid[:, 1, f, :], gact[:, n % 2, :], hid[:, 0, f, :].bitcast(F32),
                                    ALU.subtract).then_inc(s_lo, 1)

            def shared_end(q):
                for i in range(SG * q, SG * (q + 1)):
                    dve.wait_ge(s_down, i + 1)
                    r = ROWS[i]
                    v.tensor_tensor(base[0:r, i, :], base[0:r, i, :], ps[0:r, i % 2, 0:D], ALU.add).then_inc(s_base, 1)

            dve.wait_ge(slots_init, 16)
            shared_parts(0)

            dve.wait_ge(r_prefix, 1)
            link(v.tensor_copy(rtab[:, 0, :], ps[:, 6, NE * NT:NE * (NT + 1)]))
            c3 = rcmp[:, :].rearrange("p (e k) -> p e k", k=CAP)
            link(v.tensor_tensor(c3, rtab[:, 0, :].unsqueeze(2).to_broadcast([P, NE, CAP]),
                                 small[:, S_THR:S_THR + CAP].unsqueeze(1).to_broadcast([P, NE, CAP]), ALU.is_gt))
            link(v.tensor_reduce(rtab[:, 1, :], c3, AX.X, ALU.add))
            link(v.tensor_tensor_scan(rtab[:, 2, :], small[:, S_ONE:S_ONE + NE], rtab[:, 1, :], 0.0, ALU.mult, ALU.add))
            link(v.tensor_tensor(rtab[:, 3, :], rtab[:, 2, :], rtab[:, 1, :], ALU.subtract))
            link(v.tensor_scalar(rtab[:, 3, :], rtab[:, 3, :], float(P), None, ALU.mult))
            link(v.tensor_tensor(n3(rout[:, 5, :]), n3(ps[:, 6, 0:NE * NT]),
                                 rtab[:, 3, :].unsqueeze(1).to_broadcast([P, NT, NE]), ALU.add))
            for k in range(2):
                link(v.tensor_tensor(rout[:, 6 + k, :], rout[:, 5, :], rpick[:, k, :], ALU.mult))
                link(v.tensor_reduce(rsm[:, k, :], n3(rout[:, 6 + k, :]), AX.X, ALU.add))
                link(v.tensor_copy(slot_i[:, k, :], rsm[:, k, :]))
            v.tensor_copy(tend_int[:, :], rtab[0:1, 2, :]).then_inc(r_slots, 1)
            e3 = ecmp[:, :].rearrange("p (t e) -> p t e", e=NE)
            link(v.tensor_tensor(e3, small[:, S_TILE:S_TILE + TILES].unsqueeze(2).to_broadcast([P, TILES, NE]),
                                 rtab[:, 2, :].unsqueeze(1).to_broadcast([P, TILES, NE]), ALU.is_ge))
            link(v.tensor_reduce(etab[:, :], e3, AX.X, ALU.add))
            link(v.tensor_scalar(etab[:, :], etab[:, :], float(NE - 1), None, ALU.min))
            link(v.tensor_copy(e_int[:, :], etab[0:1, :]))
            link(v.tensor_scalar(ekeep[:, 0, :], etab[0:1, :], float(RING - 1), float(-RING), ALU.is_ge, ALU.mult))
            link(v.tensor_scalar(ekeep[:, 1, :], etab[0:1, :], float(2 * RING - 1), float(-RING), ALU.is_ge, ALU.mult))
            link(v.tensor_tensor(ekeep[:, 0, :], ekeep[:, 0, :], ekeep[:, 1, :], ALU.add))
            v.scalar_tensor_tensor(out=ering[:, :], in0=etab[0:1, :], scalar=1.0, in1=ekeep[:, 0, :],
                                   op0=ALU.add, op1=ALU.add).then_inc(r_tiles, 1)

            shared_end(0)
            for q in range(1, NSG):
                shared_parts(q)
                shared_end(q)

            def step(s, c, first=False, x=True, up=True, tr=True):
                if x:
                    dve.wait_ge(x_in[c], 8 * s + (32 - 8 * c))
                    et = etab[:, bass.ds(s + 2, 1)]
                    if not (first and s < 0):
                        dve.wait_ge(x_meta, s + 1)
                    v.scalar_tensor_tensor(out=junk[:, c, :], in0=xg[:, c, C_EXP:C_EXP + 2], scalar=et,
                                           in1=xg[:, c, C_GATE:C_GATE + 2], op0=ALU.is_equal, op1=ALU.mult,
                                           accum_out=gate[:, bass.ds(s + 2, 1)])
                    v.tensor_scalar(dest[:, bass.ds(s + 2, 1)], xg[:, c, C_EXP + 1:C_EXP + 2], et,
                                    xg[:, c, C_TOK2:C_TOK2 + 1], ALU.is_equal, ALU.add).then_inc(x_meta, 1)
                    dve.wait_ge(x_hi, s + 3)
                    v.tensor_tensor(xgT[:, c, 1, :, :], ps[:, 4, 0:KD * P].rearrange("p (k t) -> p k t", k=KD),
                                    xgT[:, c, 0, :, :].bitcast(F32), ALU.subtract).then_inc(x_lo, 1)
                if tr:
                    for half in range(2):
                        dve.wait_ge(e_hi, 2 * s + (1 + half))
                        v.tensor_tensor(hgT[:, c, 1, 4 * half:4 * half + 4, :],
                                        ps[:, 2 + half, :].rearrange("p (k t) -> p k t", k=4),
                                        hgT[:, c, 0, 4 * half:4 * half + 4, :].bitcast(F32),
                                        ALU.subtract).then_inc(e_lo, 1)
                if not (first and s < 1):
                    dve.wait_ge(ffn_done, s + 1)
                    dve.wait_ge(x_meta, s)
                    v.tensor_scalar(y_all[:, bass.ds(s - 1, 1), :].rearrange("p a d -> p (a d)"), ps[:, 5, 0:D],
                                    gate[:, bass.ds(s - 1, 1)], None, ALU.mult).then_inc(y_ready, 1)

            run_steps(dve, step)

            for i in range(NT):
                r = ROWS[i]
                dve.wait_ge(z_in[i % 3], 16 * (i // 3 + 1))
                if i >= 3:
                    dve.wait_ge(o_out, 16 * (i - 2))
                link(v.tensor_tensor(fin[0:r, i % 3, :], zt[0:r, i % 3, 0:D], base[0:r, i, :], ALU.add))
                v.tensor_tensor(fin[0:r, i % 3, :], fin[0:r, i % 3, :], zt[0:r, i % 3, D:2 * D],
                                ALU.add).then_inc(o_ready, 1)


def kernel(**inputs):
    import numpy as np
    import concourse.bacc as bacc
    from concourse.bass_utils import run_bass_kernel_spmd

    a = {k.removeprefix("L0_"): np.asarray(v) for k, v in inputs.items()}
    f32 = np.float32
    side, ps = 6, 16

    patches = a["x"].reshape(NB, 3, side, ps, side, ps).transpose(0, 2, 4, 3, 5, 1).reshape(NB * NPATCH, PATCH)
    halves = np.concatenate([np.arange(0, D, 2), np.arange(1, D, 2)])
    up = np.concatenate([a["ffn_shared_up"], a["ffn_routed_up"]])
    down = np.concatenate([a["ffn_shared_down"], a["ffn_routed_down"]])

    k = np.arange(P)
    mats = np.stack([np.eye(P), k[:, None] < k[None, :], np.ones((P, P))], 1).astype(f32)
    tok = P * np.arange(NT + 1)[None, :] + k[:, None]
    tok[:, NT] = T + k
    row = lambda x: np.broadcast_to(np.asarray(x)[None, :], (P, len(x)))
    small = np.concatenate([tok[:, :NT] < T, row(NE - np.arange(NE)), row(P * np.arange(CAP)), row(np.arange(TILES)),
                            2 * tok, row(np.ones(NE))], 1).astype(f32)
    omega = (1.0 / f32(10000.0) ** (np.arange(D // 4, dtype=f32) / f32(D // 4 - 1))).astype(f32)
    yy, xx = np.meshgrid(np.arange(side), np.arange(side), indexing="ij")
    ya, xa = (v.reshape(-1)[:, None].astype(f32) * omega[None, :] for v in (yy, xx))
    pe = np.concatenate([np.sin(xa), np.cos(xa), np.sin(ya), np.cos(ya)], 1).astype(f32)
    pe = pe[np.arange(NB * NPATCH) % NPATCH].reshape(NTOK, TOK, D).transpose(1, 0, 2)
    theta = np.power(f32(10000.0), (f32(-2.0) * (np.arange(D // 2, dtype=f32) - f32(1.0)) / f32(D)).astype(f32)).astype(f32)
    angle = theta[:, None] * np.arange(SEQ, dtype=f32)[None, :]
    rope = np.stack([np.cos(angle), np.sin(angle)], 1).astype(f32)

    arrays = {
        "patches": patches, "txt": a["txt"], "cls_token": a["tok_cls_token"].reshape(1, D),
        "cls_pos": a["tok_cls_pos_embedding"].reshape(1, D), "ln1_gb": np.stack([a["tok_ln1_g"], a["tok_ln1_b"]]).reshape(2, KP, P).transpose(2, 0, 1),
        "tok_w": a["tok_W"], "tok_bias": a["tok_bias"], "ln2_g": a["tok_ln2_g"], "ln2_b": a["tok_ln2_b"],
        "wq": a["attn_wq"][halves].T, "wk": a["attn_wk"][halves].T, "wv": a["attn_wv"].T,
        "w_up": up.reshape(NX, KD, P, F).transpose(0, 2, 1, 3).reshape(NX, P, UPW),
        "w_dn": down.reshape(NX, KF, P, D).transpose(0, 2, 1, 3).reshape(NX, P, UPW),
        "router_w": a["ffn_router_w"], "c_mats": mats, "c_small": small, "c_pe": pe, "c_rope": rope,
    }
    nc = bacc.Bacc("TRN2", target_bir_lowering=False, num_devices=1)
    data, args = {}, {}
    for name, v in arrays.items():
        data[f"in_{name}"] = np.ascontiguousarray(v)
        args[name] = nc.dram_tensor(f"in_{name}", v.shape, F32, kind="ExternalInput").ap()
    args["out"] = nc.dram_tensor("out_tokens", (T, D), F32, kind="ExternalOutput").ap()
    fusion_layer(nc, **args)
    r = run_bass_kernel_spmd(nc, [data], core_ids=[0])
    return r.results[0]["out_tokens"].reshape(NB, SEQ, D)
```

```python
from contextlib import ExitStack

import concourse.bass as bass
from concourse import mybir

F32 = mybir.dt.float32
F32R = mybir.dt.float32r
I32 = mybir.dt.int32
U32 = mybir.dt.uint32
ALU = mybir.AluOpType
ACT = mybir.ActivationFunctionType
AX = mybir.AxisListType

P = 128
NB, NPATCH, NTXT, D, F, NE = 16, 36, 32, 256, 1024, 8
SEQ = 1 + NPATCH + NTXT
T = NB * SEQ
PATCH = 768
EPS = 1e-5
KD = D // P
KF = F // P
TOK = 96
NTOK = NB * NPATCH // TOK
KP = PATCH // P
GB = 4
NG = NB // GB
GT = GB * SEQ
QSCALE = 1.0 / 16.0
NT = -(-T // P)
TPAD = NT * P
ROWS = [min(P, T - P * i) for i in range(NT)]
SG = 3
NSG = NT // SG
SN = SG * P
TILES = (2 * T - NE) // P + NE
XW = D + 5
C_TOK2, C_EXP, C_GATE = D, D + 1, D + 3
CAP = -(-T // P)
RING = 3
EW = 2 * KD * F
UPW = KD * F
NX = NE + 1

S_VALID, S_RANK, S_THR, S_TILE = 0, NT, NT + NE, NT + NE + CAP
S_TOK2 = S_TILE + TILES
S_ONE = S_TOK2 + NT + 1
NSMALL = S_ONE + NE


def fusion_layer(nc, patches, txt, cls_token, cls_pos, ln1_gb, tok_w, tok_bias, ln2_g, ln2_b,
                 wq, wk, wv, w_up, w_dn, router_w, c_mats, c_small, c_pe, c_rope, out):
    ctx = ExitStack()
    early = ExitStack()
    shared = ExitStack()

    def sb(name, shape, dt=F32, where=ctx, side="left"):
        return where.enter_context(nc.sbuf_tensor(name, shape, dt, side=side))

    def sem(name):
        return ctx.enter_context(nc.semaphore(name))

    img_d = nc.dram_tensor("img_tokens", [NB * NPATCH, D], F32).ap()
    h2_d = nc.dram_tensor("h_after_attention", [T, D], F32).ap()
    slots_d = nc.dram_tensor("slots", [TILES * P, XW], F32).ap()
    z_d = nc.dram_tensor("gated_outputs", [2 * T, D], F32).ap()

    with ctx:
        mats = sb("mats", [P, 3, P])
        ident, upper, ones = mats[:, 0, :], mats[:, 1, :], mats[:, 2, :]
        small = sb("small", [P, NSMALL])
        half_neg = sb("half_neg", [P, NT])
        hx = sb("hx", [P, NT, XW])
        base = sb("base", [P, NT, D])
        stage = sb("stage", [P, 2, UPW])
        gact = sb("gact", [P, 2, SN])
        hT_n = sb("hT_n", [P, 2, KD, TPAD], F32R, shared, "right")
        hid = sb("hid", [P, 2, KF, SN], F32R, shared, "right")
        shared.close()
        rout = sb("rout", [P, 8, NT * NE])
        rsm = sb("rsm", [P, 8, NT])
        rtab = sb("rtab", [P, 4, NE])
        rpick = sb("rpick", [P, 2, NT * NE])
        rsel = sb("rsel", [P, (NT + 1) * NE])
        rcmp = sb("rcmp", [P, NE * CAP])
        etab = sb("etab", [P, TILES])
        ecmp = sb("ecmp", [P, TILES * NE])
        eplace = sb("eplace", [1, TILES], I32)
        ekeep = sb("ekeep", [1, 2, TILES])
        tend_int = sb("tend_int", [1, NE], I32)
        slot_i = sb("slot_i", [P, 2, NT], I32)
        rw = sb("rw", [P, KD, NE])
        rws = sb("rws", [P, 2, KD, NE], F32R)
        st2 = sb("st2", [P, NT, 6])
        mv2 = sb("mv2", [P, NT, 2])
        rs2 = sb("rs2", [P, NT])
        h2f = sb("h2f", [P, 2, D])
        ring0_pad = early.enter_context(nc.sbuf_tensor("ring0_pad", [P, 2 * EW], F32))

        xp = sb("xp", [TOK, NTOK, PATCH], where=early)
        tw = sb("tw", [P, KP, D], where=early)
        lngb = sb("lngb", [P, 2, KP], where=early)
        xT = sb("xT", [P, 2, KP, TOK], where=early)
        tt = sb("tt", [TOK, 3, D], where=early)
        pe = sb("pe", [TOK, NTOK, D], where=early)
        vecs = sb("vecs", [TOK, 3, D], where=early)
        tst = sb("tst", [TOK, 2 * NTOK, 12], where=early)
        tmv = sb("tmv", [TOK, 2 * NTOK, 2], where=early)
        trs = sb("trs", [TOK, 2 * NTOK], where=early)
        clsr = sb("clsr", [1, 3, D], where=early)
        wqk = sb("wqk", [P, 2, KD, D], where=early)
        wvs = sb("wvs", [P, KD, D], where=early)
        rope = sb("rope", [P, 2, SEQ], where=early)
        h = sb("h", [SEQ, NB, D], where=early)
        hn = sb("hn", [SEQ, GB, D], where=early)
        ast = sb("ast", [SEQ, NG, GB, 6], where=early)
        amv = sb("amv", [SEQ, NG, GB, 2], where=early)
        ars = sb("ars", [SEQ, NG, GB], where=early)
        anb = sb("anb", [SEQ, NG, GB], where=early)
        hT = sb("hT", [P, KD, GT], where=early)
        qks = sb("qks", [P, 2, 2, GT], where=early)
        qsin = sb("qsin", [P, 2, 2, GT], where=early)
        qk = sb("qk", [P, 2, 2, GT], where=early)
        sc = sb("sc", [SEQ, GB, SEQ], where=early)
        pr = sb("pr", [SEQ, GB, SEQ], where=early)
        asm = sb("asm", [SEQ, 3, GB], where=early)
        prT = sb("prT", [SEQ, GB, SEQ], where=early)
        vv = xp[0:SEQ, 0:3, :].rearrange("p n w -> p (n w)")[:, 0:2 * GB * D].rearrange(
            "p (u b d) -> p u b d", u=2, b=GB)
        early.close()

        ring = sb("ring", [P, RING, 2, EW], F32R)
        xg = sb("xg", [P, 2, XW])
        xgT = sb("xgT", [P, 2, 2, KD, P], F32R)
        hg = sb("hg", [P, 2, F])
        hgT = sb("hgT", [P, 2, 2, KF, P], F32R, side="right")
        gate = sb("gate", [P, TILES])
        junk = sb("junk", [P, 2, 2])
        dest = sb("dest", [P, TILES], I32)
        y_all = sb("y_all", [P, TILES, D], side="right")
        zt = [stage[:, :, :].rearrange("p a n -> p (a n)")[:, 2 * D * i:2 * D * (i + 1)] for i in range(NT - 1)]
        zt.append(hx[:, :, :].rearrange("p n w -> p (n w)")[:, 0:2 * D])

        ps = ctx.enter_context(nc.psum_tensor("ps", [P, 8, 512], F32))

        patches_in = [sem(f"patches_in{i}") for i in range(NTOK)]
        tok_w_in, tok_vec_in, consts_in = sem("tok_w_in"), sem("tok_vec_in"), sem("consts_in")
        attn_w_in, cls_in, router_in = sem("attn_w_in"), sem("cls_in"), sem("router_in")
        s_dve = sem("dve_chain")
        s_pool = sem("pool_chain")
        t_stats, t_rstd = sem("t_stats"), sem("t_rstd")
        t_normed, t_tr, t_aff, t_norm2 = sem("t_normed"), sem("t_tr"), sem("t_aff"), sem("t_norm2")
        t_mm, t_stats2, t_rstd2, t_done = sem("t_mm"), sem("t_stats2"), sem("t_rstd2"), sem("t_done")
        cls_ready, first_in = sem("cls_ready"), sem("first_in")
        pe_in, rope_in, text_in = sem("pe_in"), sem("rope_in"), sem("text_in")
        img_out = [sem(f"img_out{i}") for i in range(NTOK)]
        h_in = [sem(f"h_in{i}") for i in range(NG)]
        a_stats, a_rstd, a_normed, a_tr, a_hT = (sem(n) for n in ("a_stats", "a_rstd", "a_normed", "a_tr", "a_hT"))
        a_norm_in = sem("a_norm_in")
        a_qks, a_sin = sem("a_qks"), sem("a_sin")
        a_qk, a_rope, a_v, a_vs = (sem(n) for n in ("a_qk", "a_rope", "a_v", "a_vs"))
        a_scores, a_sub, a_exp, a_pT, a_pTs = (sem(n) for n in ("a_scores", "a_sub", "a_exp", "a_pT", "a_pTs"))
        a_pv, a_h2 = sem("a_pv"), sem("a_h2")
        h2_out = [sem(f"h2_out{i}") for i in range(NG)]
        f_in = [sem(f"f_in{i}") for i in range(2)]
        f_stats, f_rstd, f_normed, f_base, f_tr, f_hi, f_lo = (
            sem(n) for n in ("f_stats", "f_rstd", "f_normed", "f_base", "f_tr", "f_hi", "f_lo"))
        pads, rws_ready, logits = sem("pads"), sem("rws_ready"), sem("logits")
        r_sub, r_exp, r_mask, r_prefix, r_slots, r_tiles = (
            sem(n) for n in ("r_sub", "r_exp", "r_mask", "r_prefix", "r_slots", "r_tiles"))
        slot_free = sem("slot_free")
        empty_row = sem("empty_row")
        slots_init, slots_out = sem("slots_init"), sem("slots_out")
        w_in = [sem(f"w_in{i}") for i in range(2)]
        w_free, w_ready = sem("w_free"), sem("w_ready")
        s_up, s_act, s_hi, s_lo, s_down, s_base = (
            sem(n) for n in ("s_up", "s_act", "s_hi", "s_lo", "s_down", "s_base"))
        x_in = [sem(f"x_in{i}") for i in range(2)]
        x_tr, x_meta, x_hi, x_lo = sem("x_tr"), sem("x_meta"), sem("x_hi"), sem("x_lo")
        e_up, e_act, e_tr, e_hi, e_lo = (sem(n) for n in ("e_up", "e_act", "e_tr", "e_hi", "e_lo"))
        ffn_done, y_ready, z_out = sem("ffn_done"), sem("y_ready"), sem("z_out")
        z_in = [sem(f"z_in{i}") for i in range(NT)]
        o_ready, o_out = sem("o_ready"), sem("o_out")

        needs = [-(-(P * i + ROWS[i]) // GT) for i in range(NT)]

        def flat_tiles_after(g):
            return [i for i in range(NT) if needs[i] == g]

        flat_bank = [2 + i % 2 if needs[i] < NG - 1 else i % 2 for i in range(NT)]

        block = ctx.enter_context(nc.Block())

        def run_steps(eng, step):
            for s in range(-2, 3):
                step(s, s % 2, first=True, up=s >= -1, tr=s >= 0)
            pairs = (TILES - 2 - 3) // 2
            with eng.Fori(0, pairs) as i:
                for c in range(2):
                    step(2 * i + (3 + c), (3 + c) % 2)
            for s in range(3 + 2 * pairs, TILES + 1):
                step(s, s % 2, x=s + 2 < TILES, up=s + 1 < TILES, tr=s < TILES)

        @block.sync
        def _(sp):
            for i in range(NTOK):
                sp.dma_start(xp[:, i, :], patches[TOK * i:TOK * (i + 1), :]).then_inc(patches_in[i], 16)
            sp.dma_start(h[1 + NPATCH:SEQ, :, :], txt.rearrange("b s d -> s b d")).then_inc(text_in, 16)
            sp.wait_ge(cls_ready, 1)
            sp.dma_start(h[0:1, :, :], clsr[0:1, 2:3, :].to_broadcast([1, NB, D])).then_inc(text_in, 16)

            g = 0
            for i in range(NTOK):
                sp.wait_ge(t_done, i + 1)
                sp.dma_start(img_d[TOK * i:TOK * (i + 1), :], tt[:, i % 3, :]).then_inc(img_out[i], 16)
                while g < NG and NPATCH * GB * (g + 1) <= TOK * (i + 1):
                    for j in range(i + 1):
                        sp.wait_ge(img_out[j], 16)
                    sp.dma_start(h[1:1 + NPATCH, GB * g:GB * (g + 1), :],
                                 img_d[NPATCH * GB * g:NPATCH * GB * (g + 1), :].rearrange("(b s) d -> s b d", s=NPATCH)
                                 ).then_inc(h_in[g], 16)
                    g += 1
            sp.wait_ge(empty_row, 1)
            sp.dma_start(slots_d.rearrange("(t p) w -> p t w", p=P),
                         gact[:, 0:1, 0:XW].to_broadcast([P, TILES, XW])).then_inc(slots_init, 16)
            for g in range(NG):
                sp.wait_ge(a_h2, g + 1)
                sp.dma_start(h2_d[GT * g:GT * (g + 1), :].rearrange("(b s) d -> s b d", s=SEQ),
                             h[:, GB * g:GB * (g + 1), :]).then_inc(h2_out[g], 16)
                sp.wait_ge(h2_out[g], 16)
                for i in flat_tiles_after(g + 1):
                    if i >= 2:
                        sp.wait_ge(f_base, i - 1)
                        sp.wait_ge(f_normed, i - 1)
                    sp.dma_start(h2f[0:ROWS[i], i % 2, :], h2_d[P * i:P * i + ROWS[i], :]).then_inc(f_in[i % 2], 16)

            sp.wait_ge(slots_out, 16 * 2 * NT)
            for t in range(2):
                sp.dma_start(xg[:, t, :], slots_d[P * t:P * (t + 1), :]).then_inc(x_in[t], 16)
            with sp.Fori(0, (TILES - 3) // 2) as i:
                for c in range(2):
                    sp.wait_ge(x_tr, 2 * i + (1 + c))
                    sp.wait_ge(x_meta, 2 * i + (1 + c))
                    sp.dma_start(xg[:, c, :], slots_d[bass.ds(2 * P * i + P * (2 + c), P), :]).then_inc(x_in[c], 16)
            t = TILES - 1
            sp.wait_ge(x_tr, t - 1)
            sp.wait_ge(x_meta, t - 1)
            sp.dma_start(xg[:, t % 2, :], slots_d[P * t:P * (t + 1), :]).then_inc(x_in[t % 2], 16)

            sp.wait_ge(z_out, 16 * TILES)
            for i in range(NT):
                sp.dma_start(zt[i][0:ROWS[i], :],
                             z_d[2 * P * i:2 * P * i + 2 * ROWS[i], :].rearrange("(p k) d -> p (k d)", k=2)
                             ).then_inc(z_in[i], 16)
            for i in range(NT):
                sp.wait_ge(o_ready, i + 1)
                sp.dma_start(out[P * i:P * i + ROWS[i], :], base[0:ROWS[i], i, :]).then_inc(o_out, 16)
            sp.wait_ge(o_out, 16 * NT)

        @block.gpsimd
        def _(pool):
            link_count = [0]

            def link(ins):
                link_count[0] += 1
                ins.then_inc(s_pool, 1)
                pool.wait_ge(s_pool, link_count[0])

            def load_weights(n):
                if n < 2 * NX:
                    if n >= 2:
                        pool.wait_ge(w_free, n - 1)
                    pool.dma_start(stage[:, n % 2, :], (w_up, w_dn)[n % 2][n // 2, :, :]).then_inc(w_in[n % 2], 16)

            def tiles_before(x):
                return pool.value_load(tend_int[0:1, x - 1:x], min_val=0, max_val=TILES)

            def split(x, part, c0, c1):
                pool.wait_ge(w_in[part], 16 * (x + 1))
                hi, lo = (ring[:, x % RING, v, UPW * part + c0:UPW * part + c1] for v in range(2))
                link(nc.gpsimd.tensor_scalar(hi, stage[:, part, c0:c1], 1.0, 0.0, ALU.mult, ALU.add))
                return nc.gpsimd.tensor_tensor(lo, stage[:, part, c0:c1], hi.bitcast(F32), ALU.subtract)

            def turn_done(x):
                pool.wait_ge(w_free, 2 * x + 2)
                pool.sem_inc(w_ready, 4)

            def prepare(x):
                for part in range(2):
                    load_weights(2 * x + part + 1)
                    if x >= RING and part == 0:
                        if x == RING:
                            pool.wait_ge(ffn_done, 1)
                        else:
                            pool.wait_ge(ffn_done, tiles_before(x - RING) + 1)
                        pool.sem_inc(slot_free, 1)
                    split(x, part, 0, UPW).then_inc(w_free, 1)
                turn_done(x)

            link(nc.gpsimd.memset(half_neg[:, :], -0.5))
            nc.gpsimd.memset(hT_n[:, :, :, T:TPAD].bitcast(F32), 0.0).then_inc(pads, 1)
            pool.wait_ge(cls_in, 32)
            nc.gpsimd.tensor_tensor(clsr[:, 2, :], clsr[:, 0, :], clsr[:, 1, :], ALU.add).then_inc(cls_ready, 1)

            def root(o, i, n, done):
                nc.gpsimd.tensor_tensor(o, i, half_neg[0:n, 0:o.shape[-1]], ALU.pow).then_inc(done, 1)

            def attention_root(g):
                pool.wait_ge(a_stats, g + 1)
                root(ars[:, g, :], amv[:, g, :, 1], SEQ, a_rstd)

            for k in range(NTOK + 4):
                if k < NTOK:
                    pool.wait_ge(t_stats, k + 1)
                    root(trs[:, k:k + 1], tmv[:, k, 1:2], TOK, t_rstd)
                i = k - 3
                if 0 <= i < NTOK:
                    pool.wait_ge(t_stats2, i + 1)
                    root(trs[:, NTOK + i:NTOK + i + 1], tmv[:, NTOK + i, 1:2], TOK, t_rstd2)
                if k == NTOK + 2:
                    attention_root(0)
                i = k - 4
                if 0 <= i < NTOK:
                    if i == 0:
                        pool.wait_ge(tok_vec_in, 48)
                        pool.wait_ge(pe_in, 16)
                    pool.wait_ge(t_norm2, i + 1)
                    o = tt[:, i % 3, :]
                    link(nc.gpsimd.tensor_tensor(o, o, vecs[:, 1, :], ALU.mult))
                    link(nc.gpsimd.tensor_tensor(o, o, vecs[:, 2, :], ALU.add))
                    nc.gpsimd.tensor_tensor(o, o, pe[:, i, :], ALU.add).then_inc(t_done, 1)
                if k == 0:
                    load_weights(0)
                    load_weights(1)

            def attention_sin(g):
                if g == 0:
                    pool.wait_ge(rope_in, 16)
                if g >= 1:
                    pool.wait_ge(a_rope, g)
                for n in (1, 0):
                    pool.wait_ge(a_qks, 2 * g + 2 - n)
                    last = nc.gpsimd.tensor_tensor(
                        qsin[:, n, :, :].rearrange("p w (b s) -> p (w b) s", b=GB),
                        qks[:, n, :, :].rearrange("p w (b s) -> p (w b) s", b=GB),
                        rope[:, 1:2, :].to_broadcast([P, 2 * GB, SEQ]), ALU.mult)
                    last.then_inc(a_sin, 1)

            def flat_roots(g):
                for i in flat_tiles_after(g):
                    pool.wait_ge(f_stats, i + 1)
                    root(rs2[0:ROWS[i], i:i + 1], mv2[0:ROWS[i], i, 1:2], ROWS[i], f_rstd)
                for i in flat_tiles_after(g):
                    pool.wait_ge(f_normed, i + 1)
                    r = ROWS[i]
                    nc.gpsimd.tensor_tensor(base[0:r, i, :], h2f[0:r, i % 2, :], hx[0:r, i, 0:D], ALU.add).then_inc(f_base, 1)

            def shared_piece(n):
                last = split(0, n // 2, UPW // 2 * (n % 2), UPW // 2 * (n % 2 + 1))
                if n % 2:
                    last.then_inc(w_free, 1)
                if n == 3:
                    turn_done(0)

            attention_sin(0)
            attention_root(1)
            shared_piece(0)
            for g in range(NG):
                if g + 1 < NG:
                    attention_sin(g + 1)
                if g + 2 < NG:
                    attention_root(g + 2)
                flat_roots(g)
                if g < 3:
                    shared_piece(g + 1)
            load_weights(2)
            for i in flat_tiles_after(NG):
                pool.wait_ge(f_stats, i + 1)
                root(rs2[0:ROWS[i], i:i + 1], mv2[0:ROWS[i], i, 1:2], ROWS[i], f_rstd)
                pool.wait_ge(f_normed, i + 1)
                r = ROWS[i]
                nc.gpsimd.tensor_tensor(base[0:r, i, :], h2f[0:r, i % 2, :], hx[0:r, i, 0:D], ALU.add).then_inc(f_base, 1)

            pool.wait_ge(a_h2, NG)
            for g in range(NG):
                pool.wait_ge(h2_out[g], 16)
            prepare(1)
            pool.wait_ge(slots_init, 16)
            pool.wait_ge(r_slots, 1)
            for i in range(NT):
                for k in range(2):
                    pool.indirect_dma_start(
                        slots_d, bass.IndirectOffsetOnAxis(ap=slot_i[0:ROWS[i], k, i:i + 1].bitcast(U32), axis=0),
                        hx[0:ROWS[i], i, :], None).then_inc(slots_out, 16)
            prepare(2)
            for x in range(RING, NX):
                prepare(x)
            for t in range(TILES):
                pool.wait_ge(y_ready, t + 1)
                pool.indirect_dma_start(z_d, bass.IndirectOffsetOnAxis(ap=dest[:, t:t + 1].bitcast(U32), axis=0),
                                        y_all[:, t, :], None, bounds_check=2 * T - 1, oob_is_err=False
                                        ).then_inc(z_out, 16)

        @block.scalar
        def _(act):
            act.dma_start(mats[:, :, :], c_mats).then_inc(first_in, 16)
            act.dma_start(lngb[:, :, :], ln1_gb).then_inc(first_in, 16)
            act.dma_start(tw[:, :, :], tok_w.rearrange("(k p) d -> p k d", p=P)).then_inc(tok_w_in, 16)
            for n, v in enumerate((tok_bias, ln2_g, ln2_b)):
                act.dma_start(vecs[:, n, :], v.partition_broadcast(TOK)).then_inc(tok_vec_in, 16)
            act.dma_start(clsr[:, 0, :], cls_token).then_inc(cls_in, 16)
            act.dma_start(clsr[:, 1, :], cls_pos).then_inc(cls_in, 16)
            act.dma_start(pe[:, :, :], c_pe).then_inc(pe_in, 16)
            act.dma_start(wqk[:, 0, :, :], wq.rearrange("(k p) d -> p k d", p=P)).then_inc(attn_w_in, 16)
            act.dma_start(wqk[:, 1, :, :], wk.rearrange("(k p) d -> p k d", p=P)).then_inc(attn_w_in, 16)
            act.dma_start(wvs[:, :, :], wv.rearrange("(k p) d -> p k d", p=P)).then_inc(attn_w_in, 16)
            act.dma_start(rope[:, :, :], c_rope).then_inc(rope_in, 16)
            act.dma_start(small[:, :], c_small).then_inc(consts_in, 16)
            act.dma_start(rw[:, :, :], router_w.rearrange("(k p) e -> p k e", p=P)).then_inc(router_in, 16)

            act.wait_ge(first_in, 32)
            for i in range(NTOK):
                act.wait_ge(t_tr, i + 1)
                if i >= 2:
                    act.wait_ge(t_mm, i - 1)
                for c in range(KP):
                    last = nc.scalar.activation(xT[:, i % 2, c, :],
                                                ps[:, 2 * (i % 2) + c // 3, TOK * (c % 3):TOK * (c % 3 + 1)],
                                                ACT.Identity, bias=lngb[:, 1, c:c + 1], scale=lngb[:, 0, c:c + 1])
                last.then_inc(t_aff, 1)

            def attention_norm(g):
                act.wait_ge(a_rstd, g + 1)
                act.wait_ge(a_norm_in, g + 1)
                if g >= 1:
                    act.wait_ge(a_tr, g)
                for b in range(GB):
                    last = nc.scalar.activation(hn[:, b, :], h[:, GB * g + b, :], ACT.Identity,
                                                bias=anb[:, g, b:b + 1], scale=ars[:, g, b:b + 1])
                last.then_inc(a_normed, 1)

            def attention_copy(g):
                act.wait_ge(a_tr, g + 1)
                if g >= 1:
                    act.wait_ge(a_v, g)
                nc.scalar.activation(hT[:, :, :], ps[:, 0:2, 0:GT], ACT.Copy).then_inc(a_hT, 1)

            def attention_halves(g):
                act.wait_ge(a_qk, g + 1)
                if g >= 1:
                    act.wait_ge(a_sin, 2 * g)
                    act.wait_ge(a_rope, g)
                for n in (1, 0):
                    nc.scalar.activation(qks[:, n, :, :], ps[:, 2 + 2 * n:4 + 2 * n, 0:GT], ACT.Copy).then_inc(a_qks, 1)

            def attention_values(g):
                act.wait_ge(a_v, g + 1)
                if g >= 2:
                    act.wait_ge(a_pv, g - 1)
                nc.scalar.activation(vv[:, g % 2, :, :].rearrange("p (a b) d -> p a (b d)", a=2),
                                     ps[0:SEQ, 6:8, :], ACT.Copy).then_inc(a_vs, 1)

            def attention_exp(g):
                act.wait_ge(a_sub, g + 1)
                if g >= 1:
                    act.wait_ge(a_pT, g)
                nc.scalar.activation(pr[:, :, :], sc[:, :, :], ACT.Exp, scale=QSCALE).then_inc(a_exp, 1)

            def flat_high(tiles):
                for i in tiles:
                    act.wait_ge(f_tr, i + 1)
                    nc.scalar.activation(hT_n[:, 0, :, P * i:P * i + ROWS[i]],
                                         ps[:, flat_bank[i], 0:KD * P].rearrange("p (k t) -> p k t", k=KD)[:, :, 0:ROWS[i]],
                                         ACT.Copy).then_inc(f_hi, 1)

            attention_norm(0)
            attention_copy(0)
            attention_halves(0)
            attention_norm(1)
            attention_values(0)
            for g in range(NG):
                flat_high(flat_tiles_after(g - 1))
                if g + 1 < NG:
                    attention_copy(g + 1)
                attention_exp(g)
                if g + 1 < NG:
                    attention_halves(g + 1)
                    attention_values(g + 1)
                if g + 2 < NG:
                    attention_norm(g + 2)

            def shared_act(n0, n1):
                for n in range(n0, n1):
                    act.wait_ge(s_up, n + 1)
                    if n >= 2:
                        act.wait_ge(s_lo, n - 1)
                    nc.scalar.activation(gact[:, n % 2, :], ps[:, 2 + n % 4, 0:SN], ACT.Gelu).then_inc(s_act, 1)

            act.wait_ge(slots_init, 16)
            shared_act(0, 4)
            flat_high(flat_tiles_after(NG - 1))
            shared_act(4, KF)
            flat_high(flat_tiles_after(NG))
            act.wait_ge(r_sub, 1)
            nc.scalar.activation(rout[:, 1, :], rout[:, 0, :], ACT.Exp).then_inc(r_exp, 1)
            shared_act(KF, NSG * KF)

            def step(s, c, first=False, x=True, up=True, tr=True):
                if x:
                    act.wait_ge(x_tr, s + 3)
                    if not (first and s < 0):
                        act.wait_ge(e_up, 2 * s + 2)
                    nc.scalar.activation(xgT[:, c, 0, :, :], ps[:, 4, 0:KD * P].rearrange("p (k t) -> p k t", k=KD),
                                         ACT.Copy).then_inc(x_hi, 1)
                if up:
                    if not (first and s < 1):
                        act.wait_ge(e_tr, 2 * s)
                    for half in range(2):
                        act.wait_ge(e_up, 2 * s + (3 + half))
                        nc.scalar.activation(hg[:, 1 - c, 512 * half:512 * (half + 1)], ps[:, half, :],
                                             ACT.Gelu).then_inc(e_act, 1)
                if tr:
                    if not (first and s < 2):
                        act.wait_ge(ffn_done, s)
                    for half in range(2):
                        act.wait_ge(e_tr, 2 * s + (1 + half))
                        nc.scalar.activation(hgT[:, c, 0, 4 * half:4 * half + 4, :],
                                             ps[:, 2 + half, :].rearrange("p (k t) -> p k t", k=4),
                                             ACT.Copy).then_inc(e_hi, 1)

            run_steps(act, step)

        @block.tensor
        def _(te):
            def transpose(o, i, n):
                return nc.tensor.transpose(o, i, ident[0:n, 0:n])

            def ring_place(turn):
                return nc.s_assert_within(turn % 4, 0, RING - 1,
                                          skip_runtime_bounds_check_because="eplace is made of a place in the ring")

            te.wait_ge(first_in, 32)

            def tok_transposes(i):
                te.wait_ge(t_normed, i + 1)
                if i >= 2:
                    te.wait_ge(t_aff, i - 1)
                for c in range(KP):
                    last = transpose(ps[:, 2 * (i % 2) + c // 3, TOK * (c % 3):TOK * (c % 3 + 1)],
                                     xp[:, i, P * c:P * (c + 1)], TOK)
                last.then_inc(t_tr, 1)

            def tok_product(i):
                te.wait_ge(t_aff, i + 1)
                if i >= 2:
                    te.wait_ge(t_stats2, i - 1)
                for c in range(KP):
                    last = nc.tensor.matmul(ps[0:TOK, 4 + i % 2, 0:D], xT[:, i % 2, c, :], tw[:, c, :],
                                            start=c == 0, stop=c == KP - 1)
                last.then_inc(t_mm, 1)

            tok_transposes(0)
            te.wait_ge(tok_w_in, 16)
            for i in range(NTOK):
                if i + 1 < NTOK:
                    tok_transposes(i + 1)
                tok_product(i)

            def attention_transposes(g):
                te.wait_ge(a_normed, g + 1)
                if g >= 2:
                    te.wait_ge(a_h2, g - 1)
                for b in range(GB):
                    for c in range(KD):
                        last = transpose(ps[:, c, SEQ * b:SEQ * (b + 1)], hn[:, b, P * c:P * (c + 1)], SEQ)
                last.then_inc(a_tr, 1)

            def attention_qk(g):
                te.wait_ge(a_hT, g + 1)
                if g == 0:
                    te.wait_ge(attn_w_in, 48)
                    te.wait_ge(t_stats2, NTOK)
                else:
                    te.wait_ge(a_qks, 2 * g)
                for eo in (1, 0):
                    if eo == 0:
                        ready = [i for n in range(g) for i in flat_tiles_after(n - 1) if flat_bank[i] >= 2]
                        if ready:
                            te.wait_ge(f_lo, len(ready))
                    for w in range(2):
                        for c in range(KD):
                            last = nc.tensor.matmul(ps[:, 2 + 2 * eo + w, 0:GT], wqk[:, w, c, P * eo:P * (eo + 1)],
                                                    hT[:, c, :], start=c == 0, stop=c == KD - 1)
                last.then_inc(a_qk, 1)

            def attention_v(g):
                if g >= 1:
                    te.wait_ge(a_sub, g)
                    te.wait_ge(a_pTs, g)
                for b in (2, 3, 0, 1):
                    for c in range(KD):
                        last = nc.tensor.matmul(ps[0:SEQ, 6 + b // 2, D * (b % 2):D * (b % 2 + 1)],
                                                hT[:, c, SEQ * b:SEQ * (b + 1)], wvs[:, c, :],
                                                start=c == 0, stop=c == KD - 1)
                last.then_inc(a_v, 1)

            def attention_scores(g):
                te.wait_ge(a_rope, g + 1)
                te.wait_ge(a_vs, g + 1)
                for b in range(GB):
                    for c in range(KD):
                        last = nc.tensor.matmul(ps[0:SEQ, 7, SEQ * b:SEQ * (b + 1)], qk[:, c, 0, SEQ * b:SEQ * (b + 1)],
                                                qk[:, c, 1, SEQ * b:SEQ * (b + 1)], start=c == 0, stop=c == KD - 1)
                last.then_inc(a_scores, 1)

            def attention_probs(g):
                te.wait_ge(a_exp, g + 1)
                for b in range(GB):
                    last = transpose(ps[0:SEQ, 6, SEQ * b:SEQ * (b + 1)], pr[:, b, :], SEQ)
                last.then_inc(a_pT, 1)

            def attention_out(g):
                te.wait_ge(a_pTs, g + 1)
                if g + 1 < NG:
                    te.wait_ge(a_hT, g + 2)
                for b in range(GB):
                    last = nc.tensor.matmul(ps[0:SEQ, b // 2, D * (b % 2):D * (b % 2 + 1)], prT[:, b, :],
                                            vv[:, g % 2, b, :], start=True, stop=True)
                last.then_inc(a_pv, 1)

            def flat_transposes(tiles):
                for i in tiles:
                    te.wait_ge(f_normed, i + 1)
                    if flat_bank[i] >= 2:
                        te.wait_ge(a_qks, 2 * (needs[i] + 2))
                    else:
                        te.wait_ge(a_h2, NG)
                    if i >= 2:
                        te.wait_ge(f_lo, i - 1)
                    for c in range(KD):
                        last = transpose(ps[:, flat_bank[i], P * c:P * c + ROWS[i]],
                                         hx[0:ROWS[i], i, P * c:P * (c + 1)], ROWS[i])
                    last.then_inc(f_tr, 1)

            attention_transposes(0)
            attention_qk(0)
            attention_v(0)
            attention_scores(0)
            for g in range(NG):
                flat_transposes(flat_tiles_after(g - 1))
                if g + 1 < NG:
                    attention_transposes(g + 1)
                    attention_qk(g + 1)
                attention_probs(g)
                if g + 1 < NG:
                    attention_v(g + 1)
                attention_out(g)
                if g + 1 < NG:
                    attention_scores(g + 1)

            def split_product(o, pairs):
                for n, (a, b) in enumerate(pairs):
                    nc.tensor.matmul(o, a[0], b[0], start=n == 0, stop=False)
                    nc.tensor.matmul(o, a[0], b[1], start=False, stop=False)
                    last = nc.tensor.matmul(o, a[1], b[0], start=False, stop=n == len(pairs) - 1)
                return last

            def router():
                for i in range(NT):
                    te.wait_ge(f_lo, i + 1)
                    last = split_product(ps[:, 7, NE * i:NE * (i + 1)],
                                         [([hT_n[:, v, c, P * i:P * (i + 1)] for v in range(2)],
                                           [rws[:, v, c, :] for v in range(2)]) for c in range(KD)])
                last.then_inc(logits, 1)

            def shared_up(q, f0, f1):
                te.wait_ge(f_lo, min(NT, SG * (q + 1)))
                for f in range(f0, f1):
                    n = KF * q + f
                    if n >= 4:
                        te.wait_ge(s_act, n - 3)
                    split_product(ps[:, 2 + n % 4, 0:SN],
                                  [([ring[:, 0, v, F * c + P * f:F * c + P * (f + 1)] for v in range(2)],
                                    [hT_n[:, v, c, SN * q:SN * (q + 1)] for v in range(2)]) for c in range(KD)]
                                  ).then_inc(s_up, 1)

            def shared_down(q):
                te.wait_ge(s_lo, KF * (q + 1))
                for j in range(SG):
                    i = SG * q + j
                    if i >= 2:
                        te.wait_ge(s_base, i - 1)
                    split_product(ps[:, i % 2, 0:D],
                                  [([hid[:, v, f, P * j:P * (j + 1)] for v in range(2)],
                                    [ring[:, 0, v, UPW + D * f:UPW + D * (f + 1)] for v in range(2)])
                                   for f in range(KF)]).then_inc(s_down, 1)

            te.wait_ge(w_ready, 4)
            shared_up(0, 0, 4)
            flat_transposes(flat_tiles_after(NG - 1))
            shared_up(0, 4, KF)
            flat_transposes(flat_tiles_after(NG))
            te.wait_ge(rws_ready, 1)
            te.wait_ge(pads, 1)
            te.wait_ge(a_sub, NG)
            router()
            shared_up(1, 0, 4)
            shared_down(0)
            te.wait_ge(r_mask, 1)
            te.wait_ge(a_pTs, NG)
            nc.tensor.matmul(ps[:, 6, 0:NE * (NT + 1)], upper, rsel[:, :], start=True, stop=False)
            for i in range(NT):
                last = nc.tensor.matmul(ps[:, 6, NE * (i + 1):NE * (NT + 1)].rearrange("p (n e) -> p n e", e=NE), ones,
                                        rsel[:, NE * i:NE * (i + 1)].unsqueeze(1).to_broadcast([P, NT - i, NE]),
                                        start=False, stop=i == NT - 1)
            last.then_inc(r_prefix, 1)
            shared_up(1, 4, KF)
            shared_up(2, 0, 4)
            shared_down(1)
            shared_up(2, 4, KF)
            shared_down(2)
            te.wait_ge(s_down, NT)
            te.sem_inc(ffn_done, 1)
            te.wait_ge(s_base, NT)
            te.wait_ge(r_tiles, 1)

            def step(s, c, first=False, x=True, up=True, tr=True):
                if x:
                    te.wait_ge(x_in[c], 8 * s + (32 - 8 * c))
                    if not (first and s < -1):
                        te.wait_ge(x_lo, s + 2)
                    for k in range(KD):
                        last = transpose(ps[:, 4, P * k:P * (k + 1)], xg[:, c, P * k:P * (k + 1)], P)
                    last.then_inc(x_tr, 1)
                if up:
                    te.wait_ge(x_lo, s + 2)
                    turn = te.value_load(eplace[0:1, bass.ds(s + 1, 1)], min_val=4, max_val=4 * NX + RING)
                    te.wait_ge(w_ready, turn + 1)
                    place = ring_place(turn)
                    w = ring[:, bass.ds(place, 1), :, :].rearrange("p a v n -> p (a v) n")
                    for half in range(2):
                        if not (first and s < 0):
                            te.wait_ge(e_act, 2 * s + (1 + half))
                        split_product(ps[:, half, :],
                                      [([xgT[:, 1 - c, v, k, :] for v in range(2)],
                                        [w[:, v, F * k + 512 * half:F * k + 512 * (half + 1)] for v in range(2)])
                                       for k in range(KD)]).then_inc(e_up, 1)
                if tr:
                    for half in range(2):
                        te.wait_ge(e_act, 2 * s + (1 + half))
                        if not (first and s < 1):
                            te.wait_ge(e_lo, 2 * s + (half - 1))
                        for k in range(4):
                            f = 4 * half + k
                            last = transpose(ps[:, 2 + half, P * k:P * (k + 1)], hg[:, c, P * f:P * (f + 1)], P)
                        last.then_inc(e_tr, 1)
                if not (first and s < 1):
                    te.wait_ge(e_lo, 2 * s)
                    if not (first and s < 2):
                        te.wait_ge(y_ready, s - 1)
                    turn = te.value_load(eplace[0:1, bass.ds(s - 1, 1)], min_val=4, max_val=4 * NX + RING)
                    place = ring_place(turn)
                    w = ring[:, bass.ds(place, 1), :, :].rearrange("p a v n -> p (a v) n")
                    split_product(ps[:, 5, 0:D],
                                  [([hgT[:, 1 - c, v, k, :] for v in range(2)],
                                    [w[:, v, UPW + D * k:UPW + D * (k + 1)] for v in range(2)])
                                   for k in range(KF)]).then_inc(ffn_done, 1)

            run_steps(te, step)

        @block.vector
        def _(dve):
            v = nc.vector
            link_count = [0]

            def link(ins):
                link_count[0] += 1
                ins.then_inc(s_dve, 1)
                dve.wait_ge(s_dve, link_count[0])

            def tok_stats(i):
                dve.wait_ge(patches_in[i], 16)
                for j in range(2):
                    last = v.bn_stats(tst[:, i, 6 * j:6 * j + 6], xp[:, i, 384 * j:384 * (j + 1)])
                link(last)
                link(v.bn_aggr(tmv[:, i, :], tst[:, i, :]))
                v.tensor_scalar(tmv[:, i, 1:2], tmv[:, i, 1:2], EPS, None, ALU.add).then_inc(t_stats, 1)

            def tok_norm(i):
                dve.wait_ge(t_rstd, i + 1)
                v.tensor_scalar(xp[:, i, :], xp[:, i, :], tmv[:, i, 0:1], trs[:, i:i + 1], ALU.subtract,
                                ALU.mult).then_inc(t_normed, 1)

            def tok_stats2(i):
                dve.wait_ge(t_mm, i + 1)
                if i == 0:
                    dve.wait_ge(tok_vec_in, 48)
                if i >= 3:
                    dve.wait_ge(img_out[i - 3], 16)
                n = NTOK + i
                link(v.tensor_tensor(tt[:, i % 3, :], ps[0:TOK, 4 + i % 2, 0:D], vecs[:, 0, :], ALU.add))
                link(v.bn_stats(tst[:, n, 0:6], tt[:, i % 3, :]))
                link(v.bn_aggr(tmv[:, n, :], tst[:, n, 0:6]))
                v.tensor_scalar(tmv[:, n, 1:2], tmv[:, n, 1:2], EPS, None, ALU.add).then_inc(t_stats2, 1)

            def tok_norm2(i):
                dve.wait_ge(t_rstd2, i + 1)
                v.tensor_scalar(tt[:, i % 3, :], tt[:, i % 3, :], tmv[:, NTOK + i, 0:1], trs[:, NTOK + i:NTOK + i + 1],
                                ALU.subtract, ALU.mult).then_inc(t_norm2, 1)

            cos = rope[:, 0:1, :].to_broadcast([P, 2 * GB, SEQ])

            def attention_front(g):
                dve.wait_ge(h_in[g], 16)
                if g == 0:
                    dve.wait_ge(text_in, 32)
                for b in range(GB):
                    last = v.bn_stats(ast[:, g, b, :], h[:, GB * g + b, :])
                link(last)
                for b in range(GB):
                    last = v.bn_aggr(amv[:, g, b, :], ast[:, g, b, :])
                link(last)
                v.tensor_scalar(amv[:, g, :, 1], amv[:, g, :, 1], EPS, None, ALU.add).then_inc(a_stats, 1)

            def attention_bias(g):
                dve.wait_ge(a_rstd, g + 1)
                v.scalar_tensor_tensor(out=anb[:, g, :], in0=amv[:, g, :, 0], scalar=-1.0, in1=ars[:, g, :],
                                       op0=ALU.mult, op1=ALU.mult).then_inc(a_norm_in, 1)

            def attention_rope(g):
                if g == 0:
                    dve.wait_ge(rope_in, 16)
                else:
                    dve.wait_ge(a_scores, g)
                wide = lambda x: x.rearrange("p w (b s) -> p (w b) s", b=GB)
                for n in (1, 0):
                    dve.wait_ge(a_qks, 2 * g + 2 - n)
                    last = v.tensor_tensor(wide(qk[:, n, :, :]), wide(qks[:, n, :, :]), cos, ALU.mult)
                link(last)
                dve.wait_ge(a_sin, 2 * g + 1)
                link(v.tensor_tensor(qk[:, 0, :, :], qk[:, 0, :, :], qsin[:, 1, :, :], ALU.add))
                dve.wait_ge(a_sin, 2 * g + 2)
                v.tensor_tensor(qk[:, 1, :, :], qk[:, 1, :, :], qsin[:, 0, :, :], ALU.subtract).then_inc(a_rope, 1)

            def attention_softmax(g):
                dve.wait_ge(a_scores, g + 1)
                s3 = ps[0:SEQ, 7, 0:GT].rearrange("p (b s) -> p b s", b=GB)
                link(v.tensor_reduce(asm[:, 0, :], s3, AX.X, ALU.max))
                if g >= 1:
                    dve.wait_ge(a_exp, g)
                v.tensor_tensor(sc[:, :, :], s3, asm[:, 0, :].unsqueeze(2).to_broadcast([SEQ, GB, SEQ]),
                                ALU.subtract).then_inc(a_sub, 1)

            def attention_sums(g):
                dve.wait_ge(a_exp, g + 1)
                link(v.tensor_reduce(asm[:, 1, :], pr[:, :, :], AX.X, ALU.add))
                link(v.reciprocal(asm[:, 2, :], asm[:, 1, :]))

            def attention_probs(g):
                dve.wait_ge(a_pT, g + 1)
                if g >= 1:
                    dve.wait_ge(a_pv, g)
                v.tensor_copy(prT[:, :, :], ps[0:SEQ, 6, 0:GT].rearrange("p (b s) -> p b s", b=GB)).then_inc(a_pTs, 1)

            def attention_end(g):
                dve.wait_ge(a_pv, g + 1)
                for b in range(GB):
                    last = v.scalar_tensor_tensor(
                        out=h[:, GB * g + b, :], in0=ps[0:SEQ, b // 2, D * (b % 2):D * (b % 2 + 1)],
                        scalar=asm[:, 2, b:b + 1], in1=h[:, GB * g + b, :], op0=ALU.mult, op1=ALU.add)
                last.then_inc(a_h2, 1)

            def flat_stats(i):
                r = ROWS[i]
                dve.wait_ge(f_in[i % 2], 16 * (i // 2 + 1))
                link(v.bn_stats(st2[0:r, i, :], h2f[0:r, i % 2, :]))
                link(v.bn_aggr(mv2[0:r, i, :], st2[0:r, i, :]))
                v.tensor_scalar(mv2[0:r, i, 1:2], mv2[0:r, i, 1:2], EPS, None, ALU.add).then_inc(f_stats, 1)

            def flat_norm(i):
                r = ROWS[i]
                dve.wait_ge(f_rstd, i + 1)
                v.tensor_scalar(hx[0:r, i, 0:D], h2f[0:r, i % 2, :], mv2[0:r, i, 0:1], rs2[0:r, i:i + 1], ALU.subtract,
                                ALU.mult).then_inc(f_normed, 1)

            def flat_low(tiles):
                for i in tiles:
                    r = ROWS[i]
                    dve.wait_ge(f_hi, i + 1)
                    cols = slice(P * i, P * i + r)
                    v.tensor_tensor(hT_n[:, 1, :, cols],
                                    ps[:, flat_bank[i], 0:KD * P].rearrange("p (k t) -> p k t", k=KD)[:, :, 0:r],
                                    hT_n[:, 0, :, cols].bitcast(F32), ALU.subtract).then_inc(f_lo, 1)

            for k in range(NTOK + 4):
                if k < NTOK:
                    tok_stats(k)
                if 0 <= k - 1 < NTOK:
                    tok_norm(k - 1)
                if k == NTOK + 2:
                    attention_front(0)
                if 0 <= k - 3 < NTOK:
                    tok_stats2(k - 3)
                if k == NTOK + 2:
                    attention_bias(0)
                if 0 <= k - 4 < NTOK:
                    tok_norm2(k - 4)

            attention_front(1)
            dve.wait_ge(consts_in, 16)
            link(v.memset(gact[:, 0, 0:XW], 0.0))
            v.memset(gact[:, 0, C_EXP:C_EXP + 2], -1.0)
            v.tensor_copy(gact[:, 0, C_TOK2:C_TOK2 + 1], small[:, S_TOK2 + NT:S_TOK2 + NT + 1]).then_inc(empty_row, 1)
            v.tensor_copy(hx[:, :, C_TOK2], small[:, S_TOK2:S_TOK2 + NT])
            attention_rope(0)
            attention_bias(1)
            dve.wait_ge(router_in, 16)
            link(v.tensor_copy(rws[:, 0, :, :], rw[:, :, :]))
            v.tensor_tensor(rws[:, 1, :, :], rw[:, :, :], rws[:, 0, :, :].bitcast(F32), ALU.subtract).then_inc(rws_ready, 1)

            for g in range(NG):
                attention_softmax(g)
                flat_low(flat_tiles_after(g - 1))
                attention_sums(g)
                attention_probs(g)
                if g + 1 < NG:
                    attention_rope(g + 1)
                if g + 2 < NG:
                    attention_front(g + 2)
                attention_end(g)
                for i in flat_tiles_after(g):
                    flat_stats(i)
                if g + 2 < NG:
                    attention_bias(g + 2)
                for i in flat_tiles_after(g):
                    flat_norm(i)

            def shared_parts(n0, n1):
                for n in range(n0, n1):
                    q, f = n // KF, n % KF
                    dve.wait_ge(s_act, n + 1)
                    if f == 0 and q >= 1:
                        dve.wait_ge(s_down, SG * q)
                    link(v.tensor_copy(hid[:, 0, f, :], gact[:, n % 2, :]))
                    v.tensor_tensor(hid[:, 1, f, :], gact[:, n % 2, :], hid[:, 0, f, :].bitcast(F32),
                                    ALU.subtract).then_inc(s_lo, 1)

            def shared_end(q):
                for i in range(SG * q, SG * (q + 1)):
                    dve.wait_ge(s_down, i + 1)
                    dve.wait_ge(f_base, i + 1)
                    r = ROWS[i]
                    v.tensor_tensor(base[0:r, i, :], base[0:r, i, :], ps[0:r, i % 2, 0:D], ALU.add).then_inc(s_base, 1)

            dve.wait_ge(slots_init, 16)
            shared_parts(0, 4)
            flat_low(flat_tiles_after(NG - 1))
            for i in flat_tiles_after(NG):
                flat_stats(i)
                flat_norm(i)
            shared_parts(4, KF)
            flat_low(flat_tiles_after(NG))

            n3 = lambda a: a.rearrange("p (n e) -> p n e", e=NE)
            over_e = lambda a: a.unsqueeze(2).to_broadcast([P, NT, NE])
            rank = small[:, S_RANK:S_RANK + NE].unsqueeze(1).to_broadcast([P, NT, NE])
            dve.wait_ge(logits, 1)
            lg = n3(ps[:, 7, 0:NT * NE])
            link(v.tensor_reduce(rsm[:, 0, :], lg, AX.X, ALU.max))
            v.tensor_tensor(n3(rout[:, 0, :]), lg, over_e(rsm[:, 0, :]), ALU.subtract).then_inc(r_sub, 1)
            dve.wait_ge(r_exp, 1)
            link(v.tensor_reduce(rsm[:, 1, :], n3(rout[:, 1, :]), AX.X, ALU.add))
            link(v.reciprocal(rsm[:, 2, :], rsm[:, 1, :]))
            link(v.tensor_tensor(n3(rout[:, 2, :]), n3(rout[:, 1, :]), over_e(rsm[:, 2, :]), ALU.mult))
            for k in range(2):
                pk, gk = rout[:, 2 + k, :], rsm[:, 3 + k, :]
                pick = rpick[:, k, :]
                link(v.tensor_reduce(gk, n3(pk), AX.X, ALU.max))
                link(v.tensor_tensor(n3(rout[:, 4, :]), n3(pk), over_e(gk), ALU.is_equal))
                link(v.tensor_tensor(n3(rout[:, 4, :]), n3(rout[:, 4, :]), rank, ALU.mult))
                link(v.tensor_reduce(rsm[:, 5 + k, :], n3(rout[:, 4, :]), AX.X, ALU.max))
                link(v.tensor_tensor(n3(pick), over_e(rsm[:, 5 + k, :]), rank, ALU.is_equal))
                if k == 0:
                    link(v.scalar_tensor_tensor(out=rout[:, 3, :], in0=pick, scalar=-2.0, in1=pk,
                                                op0=ALU.mult, op1=ALU.add))
            link(v.tensor_tensor(rsel[:, 0:NE * NT], rpick[:, 0, :], rpick[:, 1, :], ALU.add))
            v.memset(rsel[:, NE * NT:], 0.0)
            link(v.tensor_tensor(n3(rsel[:, 0:NE * NT]), n3(rsel[:, 0:NE * NT]),
                                 over_e(small[:, S_VALID:S_VALID + NT]), ALU.mult))
            for k in range(2):
                v.tensor_copy(hx[:, :, C_GATE + k], rsm[:, 3 + k, :])
                last = v.tensor_scalar(hx[:, :, C_EXP + k], rsm[:, 5 + k, :], -1.0, float(NE), ALU.mult, ALU.add)
            last.then_inc(r_mask, 1)

            shared_end(0)
            shared_parts(KF, KF + 4)

            dve.wait_ge(r_prefix, 1)
            link(v.tensor_copy(rtab[:, 0, :], ps[:, 6, NE * NT:NE * (NT + 1)]))
            c3 = rcmp[:, :].rearrange("p (e k) -> p e k", k=CAP)
            link(v.tensor_tensor(c3, rtab[:, 0, :].unsqueeze(2).to_broadcast([P, NE, CAP]),
                                 small[:, S_THR:S_THR + CAP].unsqueeze(1).to_broadcast([P, NE, CAP]), ALU.is_gt))
            link(v.tensor_reduce(rtab[:, 1, :], c3, AX.X, ALU.add))
            link(v.tensor_tensor_scan(rtab[:, 2, :], small[:, S_ONE:S_ONE + NE], rtab[:, 1, :], 0.0, ALU.mult, ALU.add))
            link(v.tensor_tensor(rtab[:, 3, :], rtab[:, 2, :], rtab[:, 1, :], ALU.subtract))
            link(v.tensor_scalar(rtab[:, 3, :], rtab[:, 3, :], float(P), None, ALU.mult))
            link(v.tensor_tensor(n3(rout[:, 5, :]), n3(ps[:, 6, 0:NE * NT]),
                                 rtab[:, 3, :].unsqueeze(1).to_broadcast([P, NT, NE]), ALU.add))
            for k in range(2):
                link(v.tensor_tensor(rout[:, 6 + k, :], rout[:, 5, :], rpick[:, k, :], ALU.mult))
                link(v.tensor_reduce(rsm[:, k, :], n3(rout[:, 6 + k, :]), AX.X, ALU.add))
                link(v.tensor_copy(slot_i[:, k, :], rsm[:, k, :]))
            v.tensor_copy(tend_int[:, :], rtab[0:1, 2, :]).then_inc(r_slots, 1)
            e3 = ecmp[:, :].rearrange("p (t e) -> p t e", e=NE)
            link(v.tensor_tensor(e3, small[:, S_TILE:S_TILE + TILES].unsqueeze(2).to_broadcast([P, TILES, NE]),
                                 rtab[:, 2, :].unsqueeze(1).to_broadcast([P, TILES, NE]), ALU.is_ge))
            link(v.tensor_reduce(etab[:, :], e3, AX.X, ALU.add))
            link(v.tensor_scalar(etab[:, :], etab[:, :], float(NE - 1), None, ALU.min))
            link(v.tensor_scalar(ekeep[:, 0, :], etab[0:1, :], float(RING - 1), float(-RING), ALU.is_ge, ALU.mult))
            link(v.tensor_scalar(ekeep[:, 1, :], etab[0:1, :], float(2 * RING - 1), float(-RING), ALU.is_ge, ALU.mult))
            link(v.tensor_tensor(ekeep[:, 0, :], ekeep[:, 0, :], ekeep[:, 1, :], ALU.add))
            link(v.tensor_scalar(ekeep[:, 1, :], etab[0:1, :], 5.0, 5.0, ALU.mult, ALU.add))
            v.tensor_tensor(eplace[:, :], ekeep[:, 0, :], ekeep[:, 1, :], ALU.add).then_inc(r_tiles, 1)

            shared_parts(KF + 4, 2 * KF)
            shared_end(1)
            shared_parts(2 * KF, 3 * KF)
            shared_end(2)

            def step(s, c, first=False, x=True, up=True, tr=True):
                if x:
                    dve.wait_ge(x_in[c], 8 * s + (32 - 8 * c))
                    et = etab[:, bass.ds(s + 2, 1)]
                    if not (first and s < 0):
                        dve.wait_ge(x_meta, s + 1)
                    v.scalar_tensor_tensor(out=junk[:, c, :], in0=xg[:, c, C_EXP:C_EXP + 2], scalar=et,
                                           in1=xg[:, c, C_GATE:C_GATE + 2], op0=ALU.is_equal, op1=ALU.mult,
                                           accum_out=gate[:, bass.ds(s + 2, 1)])
                    v.tensor_scalar(dest[:, bass.ds(s + 2, 1)], xg[:, c, C_EXP + 1:C_EXP + 2], et,
                                    xg[:, c, C_TOK2:C_TOK2 + 1], ALU.is_equal, ALU.add).then_inc(x_meta, 1)
                    dve.wait_ge(x_hi, s + 3)
                    v.tensor_tensor(xgT[:, c, 1, :, :], ps[:, 4, 0:KD * P].rearrange("p (k t) -> p k t", k=KD),
                                    xgT[:, c, 0, :, :].bitcast(F32), ALU.subtract).then_inc(x_lo, 1)
                if tr:
                    for half in range(2):
                        dve.wait_ge(e_hi, 2 * s + (1 + half))
                        v.tensor_tensor(hgT[:, c, 1, 4 * half:4 * half + 4, :],
                                        ps[:, 2 + half, :].rearrange("p (k t) -> p k t", k=4),
                                        hgT[:, c, 0, 4 * half:4 * half + 4, :].bitcast(F32),
                                        ALU.subtract).then_inc(e_lo, 1)
                if not (first and s < 1):
                    dve.wait_ge(ffn_done, s + 1)
                    dve.wait_ge(x_meta, s)
                    v.tensor_scalar(y_all[:, bass.ds(s - 1, 1), :].rearrange("p a d -> p (a d)"), ps[:, 5, 0:D],
                                    gate[:, bass.ds(s - 1, 1)], None, ALU.mult).then_inc(y_ready, 1)

            run_steps(dve, step)

            for i in range(NT):
                r = ROWS[i]
                dve.wait_ge(z_in[i], 16)
                link(v.tensor_tensor(base[0:r, i, :], base[0:r, i, :], zt[i][0:r, 0:D], ALU.add))
                v.tensor_tensor(base[0:r, i, :], base[0:r, i, :], zt[i][0:r, D:2 * D], ALU.add).then_inc(o_ready, 1)


def kernel(**inputs):
    import numpy as np
    import concourse.bacc as bacc
    from concourse.bass_utils import run_bass_kernel_spmd

    a = {k.removeprefix("L0_"): np.asarray(v) for k, v in inputs.items()}
    f32 = np.float32
    side, ps = 6, 16

    patches = a["x"].reshape(NB, 3, side, ps, side, ps).transpose(0, 2, 4, 3, 5, 1).reshape(NB * NPATCH, PATCH)
    halves = np.concatenate([np.arange(0, D, 2), np.arange(1, D, 2)])
    up = np.concatenate([a["ffn_shared_up"], a["ffn_routed_up"]])
    down = np.concatenate([a["ffn_shared_down"], a["ffn_routed_down"]])

    k = np.arange(P)
    mats = np.stack([np.eye(P), k[:, None] < k[None, :], np.ones((P, P))], 1).astype(f32)
    tok = P * np.arange(NT + 1)[None, :] + k[:, None]
    tok[:, NT] = T + k
    row = lambda x: np.broadcast_to(np.asarray(x)[None, :], (P, len(x)))
    small = np.concatenate([tok[:, :NT] < T, row(NE - np.arange(NE)), row(P * np.arange(CAP)), row(np.arange(TILES)),
                            2 * tok, row(np.ones(NE))], 1).astype(f32)
    omega = (1.0 / f32(10000.0) ** (np.arange(D // 4, dtype=f32) / f32(D // 4 - 1))).astype(f32)
    yy, xx = np.meshgrid(np.arange(side), np.arange(side), indexing="ij")
    ya, xa = (v.reshape(-1)[:, None].astype(f32) * omega[None, :] for v in (yy, xx))
    pe = np.concatenate([np.sin(xa), np.cos(xa), np.sin(ya), np.cos(ya)], 1).astype(f32)
    pe = pe[np.arange(NB * NPATCH) % NPATCH].reshape(NTOK, TOK, D).transpose(1, 0, 2)
    theta = np.power(f32(10000.0), (f32(-2.0) * (np.arange(D // 2, dtype=f32) - f32(1.0)) / f32(D)).astype(f32)).astype(f32)
    angle = theta[:, None] * np.arange(SEQ, dtype=f32)[None, :]
    rope = np.stack([np.cos(angle), np.sin(angle)], 1).astype(f32)

    arrays = {
        "patches": patches, "txt": a["txt"], "cls_token": a["tok_cls_token"].reshape(1, D),
        "cls_pos": a["tok_cls_pos_embedding"].reshape(1, D), "ln1_gb": np.stack([a["tok_ln1_g"], a["tok_ln1_b"]]).reshape(2, KP, P).transpose(2, 0, 1),
        "tok_w": a["tok_W"], "tok_bias": a["tok_bias"], "ln2_g": a["tok_ln2_g"], "ln2_b": a["tok_ln2_b"],
        "wq": a["attn_wq"][halves].T, "wk": a["attn_wk"][halves].T, "wv": a["attn_wv"].T,
        "w_up": up.reshape(NX, KD, P, F).transpose(0, 2, 1, 3).reshape(NX, P, UPW),
        "w_dn": down.reshape(NX, KF, P, D).transpose(0, 2, 1, 3).reshape(NX, P, UPW),
        "router_w": a["ffn_router_w"], "c_mats": mats, "c_small": small, "c_pe": pe, "c_rope": rope,
    }
    nc = bacc.Bacc("TRN2", target_bir_lowering=False, num_devices=1)
    data, args = {}, {}
    for name, v in arrays.items():
        data[f"in_{name}"] = np.ascontiguousarray(v)
        args[name] = nc.dram_tensor(f"in_{name}", v.shape, F32, kind="ExternalInput").ap()
    args["out"] = nc.dram_tensor("out_tokens", (T, D), F32, kind="ExternalOutput").ap()
    fusion_layer(nc, **args)
    r = run_bass_kernel_spmd(nc, [data], core_ids=[0])
    return r.results[0]["out_tokens"].reshape(NB, SEQ, D)
```

```python
from contextlib import ExitStack

import concourse.bass as bass
from concourse import mybir

F32 = mybir.dt.float32
F32R = mybir.dt.float32r
I32 = mybir.dt.int32
U32 = mybir.dt.uint32
ALU = mybir.AluOpType
ACT = mybir.ActivationFunctionType
AX = mybir.AxisListType

P = 128
NB, NPATCH, NTXT, D, F, NE = 16, 36, 32, 256, 1024, 8
SEQ = 1 + NPATCH + NTXT
T = NB * SEQ
PATCH = 768
EPS = 1e-5
KD = D // P
KF = F // P
TOK = 96
NTOK = NB * NPATCH // TOK
KP = PATCH // P
GB = 4
NG = NB // GB
GT = GB * SEQ
QSCALE = 1.0 / 16.0
NT = -(-T // P)
TPAD = NT * P
ROWS = [min(P, T - P * i) for i in range(NT)]
NBUF_FLAT = 3
LAG = 3
SG = 3
NSG = NT // SG
SN = SG * P
TILES = (2 * T - 1) // P + NE
XW = D + 5
C_TOK, C_EXP, C_GATE = D, D + 1, D + 3
CAP = -(-T // P)
RING = 3
EW = 2 * KD * F
UPW = KD * F
NX = NE + 1

S_VALID, S_RANK, S_THR, S_TILE = 0, NT, NT + NE, NT + NE + CAP
S_TOK = S_TILE + TILES
S_ONE = S_TOK + NT + 1
NSMALL = S_ONE + NE


def fusion_layer(nc, patches, txt, cls_token, cls_pos, ln1_gb, tok_w, tok_bias, ln2_g, ln2_b,
                 wq, wk, wv, w_up, w_dn, router_w, c_mats, c_small, c_pe, c_rope, out):
    ctx = ExitStack()
    early = ExitStack()
    shared = ExitStack()

    def sb(name, shape, dt=F32, where=ctx, side="left"):
        return where.enter_context(nc.sbuf_tensor(name, shape, dt, side=side))

    def sem(name):
        return ctx.enter_context(nc.semaphore(name))

    img_d = nc.dram_tensor("img_tokens", [NB * NPATCH, D], F32).ap()
    h2_d = nc.dram_tensor("h_after_attention", [T, D], F32).ap()
    slots_d = nc.dram_tensor("slots", [TILES * P, XW], F32).ap()

    with ctx:
        mats = sb("mats", [P, 3, P])
        ident, upper, ones = mats[:, 0, :], mats[:, 1, :], mats[:, 2, :]
        small = sb("small", [P, NSMALL])
        warm = sb("warm", [P, 1])
        half_neg = sb("half_neg", [P, NT])
        hx = sb("hx", [P, NT, XW])
        base = sb("base", [P, NT, D])
        stage = sb("stage", [P, 2, UPW])
        gact = sb("gact", [P, 2, SN])
        hT_n = sb("hT_n", [P, 2, KD, TPAD], F32R, shared, "right")
        hid = sb("hid", [P, 2, KF, SN], F32R, shared, "right")
        shared.close()
        rout = sb("rout", [P, 8, NT * NE])
        rsm = sb("rsm", [P, 8, NT])
        rtab = sb("rtab", [P, 4, NE])
        rpick = sb("rpick", [P, 2, NT * NE])
        rsel = sb("rsel", [P, (NT + 1) * NE])
        rcmp = sb("rcmp", [P, NE * CAP])
        etab = sb("etab", [P, TILES])
        ecmp = sb("ecmp", [P, TILES * NE])
        eplace = sb("eplace", [1, TILES], I32)
        ekeep = sb("ekeep", [1, 2, TILES])
        ytab = sb("ytab", [1, 2, TILES])
        additions = sb("additions", [1, TILES], I32)
        tend_int = sb("tend_int", [1, NE], I32)
        slot_i = sb("slot_i", [P, 2, NT], I32)
        rw = sb("rw", [P, KD, NE])
        lturn = sb("lturn", [NE, TPAD])
        rws = sb("rws", [P, 2, KD, NE], F32R)
        st2 = sb("st2", [P, NT, 6])
        mv2 = sb("mv2", [P, NT, 2])
        rs2 = sb("rs2", [P, NT])
        h2f = sb("h2f", [P, NBUF_FLAT, D])
        ring0 = early.enter_context(nc.sbuf_tensor("ring0", [P, 2 * EW], F32))
        n = KP * D
        tw = ring0[:, 0:n].rearrange("p (k d) -> p k d", k=KP)
        pe = ring0[0:TOK, n:n + NTOK * D].rearrange("p (i d) -> p i d", i=NTOK)
        n += NTOK * D
        wqk = ring0[:, n:n + 2 * KD * D].rearrange("p (w k d) -> p w k d", w=2, k=KD)
        n += 2 * KD * D
        wvs = ring0[:, n:n + KD * D].rearrange("p (k d) -> p k d", k=KD)

        xp = sb("xp", [TOK, NTOK, PATCH], where=early)
        lngb = sb("lngb", [P, 2, KP], where=early)
        xT = sb("xT", [P, 2, KP, TOK], where=early)
        tt = sb("tt", [TOK, 3, D], where=early)
        vecs = sb("vecs", [TOK, 3, D], where=early)
        tst = sb("tst", [TOK, 2 * NTOK, 12], where=early)
        tmv = sb("tmv", [TOK, 2 * NTOK, 2], where=early)
        trs = sb("trs", [TOK, 2 * NTOK], where=early)
        clsr = sb("clsr", [1, 3, D], where=early)
        wqk2 = sb("wqk2", [P, 2, 2, KD, D], F32R, where=early)
        wv2 = sb("wv2", [P, 2, KD, D], F32R, where=early)
        rope = sb("rope", [P, 2, SEQ], where=early)
        h = sb("h", [SEQ, NB, D], where=early)
        hn = sb("hn", [SEQ, GB, D], where=early)
        ast = sb("ast", [SEQ, NG, GB, 6], where=early)
        amv = sb("amv", [SEQ, NG, GB, 2], where=early)
        ars = sb("ars", [SEQ, NG, GB], where=early)
        anb = sb("anb", [SEQ, NG, GB], where=early)
        hT = sb("hT", [P, 2, 2, KD, GT], F32R, where=early)
        qks = sb("qks", [P, 2, 2, GT], where=early)
        qsin = sb("qsin", [P, 2, 2, GT], where=early)
        qk = sb("qk", [P, 2, 2, GT], where=early)
        sc = sb("sc", [SEQ, GB, SEQ], where=early)
        pr = sb("pr", [SEQ, GB, SEQ], where=early)
        asm = sb("asm", [SEQ, 3, GB], where=early)
        prT = sb("prT", [SEQ, GB, SEQ], where=early)
        vv = xp[0:SEQ, 0:3, :].rearrange("p n w -> p (n w)")[:, 0:2 * GB * D].rearrange(
            "p (u b d) -> p u b d", u=2, b=GB)
        early.close()

        ring = sb("ring", [P, RING, 2, EW], F32R)
        xg = sb("xg", [P, 2, XW])
        xgT = sb("xgT", [P, 2, 2, KD, P], F32R)
        hg = sb("hg", [P, 2, F])
        hgT = sb("hgT", [P, 2, 2, KF, P], F32R, side="right")
        gate = sb("gate", [P, TILES])
        junk = sb("junk", [P, 2, 2])
        dest = sb("dest", [P, TILES], I32)
        y_all = sb("y_all", [P, TILES, D], side="right")

        ps = ctx.enter_context(nc.psum_tensor("ps", [P, 8, 512], F32))

        patches_in = [sem(f"patches_in{i}") for i in range(NTOK)]
        tok_w_in, tok_vec_in, consts_in = sem("tok_w_in"), sem("tok_vec_in"), sem("consts_in")
        attn_w_in, cls_in, router_in = sem("attn_w_in"), sem("cls_in"), sem("router_in")
        s_dve = sem("dve_chain")
        s_pool = sem("pool_chain")
        half_ready = sem("half_ready")
        t_stats, t_rstd = sem("t_stats"), sem("t_rstd")
        t_normed, t_tr, t_aff, t_norm2 = sem("t_normed"), sem("t_tr"), sem("t_aff"), sem("t_norm2")
        t_mm, t_stats2, t_rstd2, t_done = sem("t_mm"), sem("t_stats2"), sem("t_rstd2"), sem("t_done")
        cls_ready, first_in = sem("cls_ready"), sem("first_in")
        pe_in, rope_in, text_in = sem("pe_in"), sem("rope_in"), sem("text_in")
        img_out = [sem(f"img_out{i}") for i in range(NTOK)]
        h_in = [sem(f"h_in{i}") for i in range(NG)]
        a_stats, a_rstd, a_normed, a_tr, a_hT = (sem(n) for n in ("a_stats", "a_rstd", "a_normed", "a_tr", "a_hT"))
        a_norm_in, a_low, a_w = sem("a_norm_in"), sem("a_low"), sem("a_w")
        a_qks, a_sin = sem("a_qks"), sem("a_sin")
        a_qk, a_rope, a_v, a_vs = (sem(n) for n in ("a_qk", "a_rope", "a_v", "a_vs"))
        a_scores, a_sub, a_exp, a_pT, a_pTs = (sem(n) for n in ("a_scores", "a_sub", "a_exp", "a_pT", "a_pTs"))
        a_pv, a_h2 = sem("a_pv"), sem("a_h2")
        h2_out = [sem(f"h2_out{i}") for i in range(NG)]
        f_in = [sem(f"f_in{i}") for i in range(NBUF_FLAT)]
        f_stats, f_rstd, f_normed, f_base, f_tr, f_hi, f_lo = (
            sem(n) for n in ("f_stats", "f_rstd", "f_normed", "f_base", "f_tr", "f_hi", "f_lo"))
        pads, rws_ready, logits = sem("pads"), sem("rws_ready"), sem("logits")
        l_turned, l_taken = sem("l_turned"), sem("l_taken")
        r_sub, r_exp, r_mask, r_prefix, r_slots, r_tiles = (
            sem(n) for n in ("r_sub", "r_exp", "r_mask", "r_prefix", "r_slots", "r_tiles"))
        slot_free = sem("slot_free")
        empty_row = sem("empty_row")
        slots_init, slots_out = sem("slots_init"), sem("slots_out")
        w_in = [sem(f"w_in{i}") for i in range(2)]
        w_free, w_ready = sem("w_free"), sem("w_ready")
        s_up, s_act, s_lo, s_down, s_base = (sem(n) for n in ("s_up", "s_act", "s_lo", "s_down", "s_base"))
        x_in = [sem(f"x_in{i}") for i in range(2)]
        x_tr, x_meta, x_hi, x_lo = sem("x_tr"), sem("x_meta"), sem("x_hi"), sem("x_lo")
        e_up, e_act, e_tr, e_hi, e_lo = (sem(n) for n in ("e_up", "e_act", "e_tr", "e_hi", "e_lo"))
        ffn_done, y_ready, y_out = sem("ffn_done"), sem("y_ready"), sem("y_out")
        r_additions = sem("r_additions")
        base_out, rows_free = sem("base_out"), sem("rows_free")

        needs = [-(-(P * i + ROWS[i]) // GT) for i in range(NT)]

        def flat_tiles_after(g):
            return [i for i in range(NT) if needs[i] == g]

        flat_bank = [2 + i % 2 if needs[i] < NG - 1 else 4 + 2 * (i % 2) for i in range(NT)]
        hidden_bank, turned_bank = 2, 0
        up_bank, down_bank = (2, 3), (0, 1, 5)

        block = ctx.enter_context(nc.Block())

        def run_steps(eng, step):
            for s in range(-1, 3):
                step(s, s % 2, first=True, x=s >= 0, tr=s >= 0)
            pairs = (TILES - 2 - 3) // 2
            with eng.Fori(0, pairs) as i:
                for c in range(2):
                    step(2 * i + (3 + c), (3 + c) % 2)
            for s in range(3 + 2 * pairs, TILES + 1):
                step(s, s % 2, x=s + 2 < TILES, up=s + 1 < TILES, tr=s < TILES)

        @block.sync
        def _(sp):
            for i in range(NTOK):
                sp.dma_start(xp[:, i, :], patches[TOK * i:TOK * (i + 1), :]).then_inc(patches_in[i], 16)
            sp.dma_start(pe[:, :, :], c_pe).then_inc(pe_in, 16)
            for n, v in enumerate((tok_bias, ln2_g, ln2_b)):
                sp.dma_start(vecs[:, n, :], v.partition_broadcast(TOK)).then_inc(tok_vec_in, 16)
            sp.dma_start(clsr[:, 0, :], cls_token).then_inc(cls_in, 16)
            sp.dma_start(clsr[:, 1, :], cls_pos).then_inc(cls_in, 16)
            sp.dma_start(h[1 + NPATCH:SEQ, :, :], txt.rearrange("b s d -> s b d")).then_inc(text_in, 16)
            for n, w in enumerate((wq, wk)):
                sp.dma_start(wqk[:, n, :, :], w.rearrange("(k p) d -> p k d", p=P)).then_inc(attn_w_in, 16)
            sp.dma_start(wvs[:, :, :], wv.rearrange("(k p) d -> p k d", p=P)).then_inc(attn_w_in, 16)
            sp.dma_start(rope[:, :, :], c_rope).then_inc(rope_in, 16)
            sp.dma_start(small[:, :], c_small).then_inc(consts_in, 16)
            sp.dma_start(rw[:, :, :], router_w.rearrange("(k p) e -> p k e", p=P)).then_inc(router_in, 16)
            sp.wait_ge(cls_ready, 1)
            sp.dma_start(h[0:1, :, :], clsr[0:1, 2:3, :].to_broadcast([1, NB, D])).then_inc(text_in, 16)

            g = 0
            for i in range(NTOK):
                sp.wait_ge(t_done, i + 1)
                sp.dma_start(img_d[TOK * i:TOK * (i + 1), :], tt[:, i % 3, :]).then_inc(img_out[i], 16)
                while g < NG and NPATCH * GB * (g + 1) <= TOK * (i + 1):
                    for j in range(i + 1):
                        sp.wait_ge(img_out[j], 16)
                    sp.dma_start(h[1:1 + NPATCH, GB * g:GB * (g + 1), :],
                                 img_d[NPATCH * GB * g:NPATCH * GB * (g + 1), :].rearrange("(b s) d -> s b d", s=NPATCH)
                                 ).then_inc(h_in[g], 16)
                    g += 1
            sp.wait_ge(empty_row, 1)
            sp.dma_start(slots_d.rearrange("(t p) w -> p t w", p=P),
                         gact[:, 0:1, 0:XW].to_broadcast([P, TILES, XW])).then_inc(slots_init, 16)
            sp.dma_start(out[T:T + P, :], gact[:, 0, 0:D]).then_inc(slots_init, 16)
            for g in range(NG):
                sp.wait_ge(a_h2, g + 1)
                sp.dma_start(h2_d[GT * g:GT * (g + 1), :].rearrange("(b s) d -> s b d", s=SEQ),
                             h[:, GB * g:GB * (g + 1), :]).then_inc(h2_out[g], 16)
                sp.wait_ge(h2_out[g], 16)
                for i in flat_tiles_after(g + 1):
                    if i >= NBUF_FLAT:
                        sp.wait_ge(f_base, i - NBUF_FLAT + 1)
                        sp.wait_ge(f_normed, i - NBUF_FLAT + 1)
                    n = i % NBUF_FLAT
                    sp.dma_start(h2f[0:ROWS[i], n, :], h2_d[P * i:P * i + ROWS[i], :]).then_inc(f_in[n], 16)

            for q in range(NSG - 1):
                sp.wait_ge(s_base, SG * (q + 1))
                sp.dma_start(out[SN * q:SN * (q + 1), :].rearrange("(i p) d -> p i d", p=P),
                             base[:, SG * q:SG * (q + 1), :]).then_inc(base_out, 16)

            sp.wait_ge(slots_out, 16 * 2 * NT)
            for t in range(2):
                sp.dma_start(xg[:, t, :], slots_d[P * t:P * (t + 1), :]).then_inc(x_in[t], 16)
            with sp.Fori(0, (TILES - 3) // 2) as i:
                for c in range(2):
                    sp.wait_ge(x_tr, 2 * i + (1 + c))
                    sp.wait_ge(x_meta, 2 * i + (1 + c))
                    sp.dma_start(xg[:, c, :], slots_d[bass.ds(2 * P * i + P * (2 + c), P), :]).then_inc(x_in[c], 16)
            t = TILES - 1
            sp.wait_ge(x_tr, t - 1)
            sp.wait_ge(x_meta, t - 1)
            sp.dma_start(xg[:, t % 2, :], slots_d[P * t:P * (t + 1), :]).then_inc(x_in[t % 2], 16)

            sp.wait_ge(y_out, 16 * TILES)

        @block.gpsimd
        def _(pool):
            link_count = [0]

            def link(ins):
                link_count[0] += 1
                ins.then_inc(s_pool, 1)
                pool.wait_ge(s_pool, link_count[0])

            def load_weights(n):
                if n < 2 * NX:
                    if n >= 2:
                        pool.wait_ge(w_free, n - 1)
                    pool.dma_start(stage[:, n % 2, :], (w_up, w_dn)[n % 2][n // 2, :, :]).then_inc(w_in[n % 2], 16)

            def tiles_before(x):
                return pool.value_load(tend_int[0:1, x - 1:x], min_val=0, max_val=TILES)

            def split(x, part, c0, c1):
                pool.wait_ge(w_in[part], 16 * (x + 1))
                hi, lo = (ring[:, x % RING, v, UPW * part + c0:UPW * part + c1] for v in range(2))
                link(nc.gpsimd.tensor_scalar(hi, stage[:, part, c0:c1], 1.0, 0.0, ALU.mult, ALU.add))
                return nc.gpsimd.tensor_tensor(lo, stage[:, part, c0:c1], hi.bitcast(F32), ALU.subtract)

            def turn_done(x):
                pool.wait_ge(w_free, 2 * x + 2)
                pool.sem_inc(w_ready, 4)

            def prepare_half(x, part):
                if x > RING and part == 0:
                    pool.wait_ge(ffn_done, tiles_before(x - RING) + 1)
                    pool.sem_inc(slot_free, 1)
                elif x == RING and part == 0:
                    pool.wait_ge(ffn_done, 1)
                split(x, part, 0, UPW).then_inc(w_free, 1)
                if part == 1:
                    turn_done(x)
                load_weights(2 * x + part + 2)

            link(nc.gpsimd.memset(half_neg[:, :], -0.5))
            pool.sem_inc(half_ready, 1)
            nc.gpsimd.memset(hT_n[:, :, :, T:TPAD].bitcast(F32), 0.0).then_inc(pads, 1)
            def root(o, i, n, done):
                nc.gpsimd.tensor_tensor(o, i, half_neg[0:n, 0:o.shape[-1]], ALU.pow).then_inc(done, 1)

            def attention_root(g):
                pool.wait_ge(a_stats, g + 1)
                root(ars[:, g, :], amv[:, g, :, 1], SEQ, a_rstd)

            for k in range(NTOK + 4):
                if k < NTOK:
                    pool.wait_ge(t_stats, k + 1)
                    root(trs[:, k:k + 1], tmv[:, k, 1:2], TOK, t_rstd)
                if k == 3:
                    pool.wait_ge(tok_vec_in, 48)
                    pool.wait_ge(pe_in, 16)
                    link(nc.gpsimd.tensor_tensor(pe[:, :, :], pe[:, :, :],
                                                 vecs[:, 2:3, :].to_broadcast([TOK, NTOK, D]), ALU.add))
                    pool.wait_ge(cls_in, 32)
                    nc.gpsimd.tensor_tensor(clsr[:, 2, :], clsr[:, 0, :], clsr[:, 1, :], ALU.add).then_inc(cls_ready, 1)
                if k == NTOK + 3:
                    attention_root(1)
                i = k - 4
                if 0 <= i < NTOK:
                    pool.wait_ge(t_norm2, i + 1)
                    o = tt[:, i % 3, :]
                    link(nc.gpsimd.tensor_tensor(o, o, vecs[:, 1, :], ALU.mult))
                    nc.gpsimd.tensor_tensor(o, o, pe[:, i, :], ALU.add).then_inc(t_done, 1)
                if k == NTOK + 1:
                    attention_root(0)
                i = k - 3
                if 0 <= i < NTOK:
                    pool.wait_ge(t_stats2, i + 1)
                    root(trs[:, NTOK + i:NTOK + i + 1], tmv[:, NTOK + i, 1:2], TOK, t_rstd2)
                if k in (1, 2):
                    load_weights(k - 1)

            def attention_sin(g):
                if g == 0:
                    pool.wait_ge(rope_in, 16)
                if g >= 1:
                    pool.wait_ge(a_rope, g)
                for n in (1, 0) if g >= 1 else (1,):
                    pool.wait_ge(a_qks, 2 * g + 2 - n)
                    nc.gpsimd.tensor_tensor(
                        qsin[:, n, :, :].rearrange("p w (b s) -> p (w b) s", b=GB),
                        qks[:, n, :, :].rearrange("p w (b s) -> p (w b) s", b=GB),
                        rope[:, 1:2, :].to_broadcast([P, 2 * GB, SEQ]), ALU.mult).then_inc(a_sin, 1 if g >= 1 else 2)

            def flat_roots(g):
                for i in flat_tiles_after(g):
                    pool.wait_ge(f_stats, i + 1)
                    root(rs2[0:ROWS[i], i:i + 1], mv2[0:ROWS[i], i, 1:2], ROWS[i], f_rstd)

            def flat_bases(g):
                for i in flat_tiles_after(g):
                    pool.wait_ge(f_normed, i + 1)
                    r = ROWS[i]
                    nc.gpsimd.tensor_tensor(base[0:r, i, :], h2f[0:r, i % NBUF_FLAT, :], hx[0:r, i, 0:D],
                                            ALU.add).then_inc(f_base, 1)

            def shared_piece(n):
                part = n // 2
                last = split(0, part, UPW // 2 * (n % 2), UPW // 2 * (n % 2 + 1))
                if n % 2:
                    last.then_inc(w_free, 1)
                    if n == 3:
                        turn_done(0)
                    load_weights(part + 2)

            attention_root(2)
            attention_sin(0)
            pool.wait_ge(a_w, 1)
            pool.wait_ge(t_mm, NTOK)
            shared_piece(0)
            attention_root(3)
            for g in range(NG):
                if g + 1 < NG:
                    attention_sin(g + 1)
                if g < NG - 2:
                    shared_piece(g + 1)
                flat_roots(g)
                if g == NG - 2:
                    shared_piece(g + 1)
                flat_bases(g)

            pool.wait_ge(a_h2, NG)
            for g in range(NG):
                pool.wait_ge(h2_out[g], 16)
            split(1, 0, 0, UPW // 2)
            flat_roots(NG)
            split(1, 0, UPW // 2, UPW).then_inc(w_free, 1)
            load_weights(4)
            flat_bases(NG)
            prepare_half(1, 1)
            pool.wait_ge(slots_init, 32)
            pool.wait_ge(r_slots, 1)
            for i in range(NT):
                for k in range(2):
                    pool.indirect_dma_start(
                        slots_d, bass.IndirectOffsetOnAxis(ap=slot_i[0:ROWS[i], k, i:i + 1].bitcast(U32), axis=0),
                        hx[0:ROWS[i], i, :], None).then_inc(slots_out, 16)
            for x in range(2, NX):
                for part in range(2):
                    prepare_half(x, part)
            pool.wait_ge(base_out, 16 * (NSG + 1))
            pool.wait_ge(r_additions, 1)
            for t in range(TILES):
                if t >= 1:
                    pool.wait_ge(y_out, pool.value_load(additions[0:1, t:t + 1], min_val=16, max_val=16 * TILES))
                    pool.sem_inc(rows_free, 1)
                pool.wait_ge(y_ready, t + 1)
                pool.indirect_dma_start(out, bass.IndirectOffsetOnAxis(ap=dest[:, t:t + 1].bitcast(U32), axis=0),
                                        y_all[:, t, :], None, compute_op=ALU.add).then_inc(y_out, 16)

        @block.scalar
        def _(act):
            act.dma_start(mats[:, :, :], c_mats).then_inc(first_in, 16)
            act.dma_start(lngb[:, :, :], ln1_gb).then_inc(first_in, 16)
            act.dma_start(tw[:, :, :], tok_w.rearrange("(k p) d -> p k d", p=P)).then_inc(tok_w_in, 16)

            act.wait_ge(half_ready, 1)
            nc.scalar.activation(warm[:, :], half_neg[:, 0:1], ACT.Identity)
            act.wait_ge(first_in, 32)
            for i in range(NTOK):
                act.wait_ge(t_tr, i + 1)
                if i >= 2:
                    act.wait_ge(t_mm, i - 1)
                for c in range(KP):
                    last = nc.scalar.activation(xT[:, i % 2, c, :],
                                                ps[:, 2 * (i % 2) + c // 3, TOK * (c % 3):TOK * (c % 3 + 1)],
                                                ACT.Identity, bias=lngb[:, 1, c:c + 1], scale=lngb[:, 0, c:c + 1])
                last.then_inc(t_aff, 1)

            def attention_norm(g):
                act.wait_ge(a_rstd, g + 1)
                act.wait_ge(a_norm_in, g + 1)
                if g >= 1:
                    act.wait_ge(a_tr, g)
                for b in range(GB):
                    last = nc.scalar.activation(hn[:, b, :], h[:, GB * g + b, :], ACT.Identity,
                                                bias=anb[:, g, b:b + 1], scale=ars[:, g, b:b + 1])
                last.then_inc(a_normed, 1)

            def attention_copy(g):
                act.wait_ge(a_tr, g + 1)
                if g >= 2:
                    act.wait_ge(a_v, g - 1)
                nc.scalar.activation(hT[:, g % 2, 0, :, :], ps[:, 0:2, 0:GT], ACT.Copy).then_inc(a_hT, 1)

            def attention_halves(g):
                act.wait_ge(a_qk, g + 1)
                if g >= 1:
                    act.wait_ge(a_sin, 2 * g)
                    act.wait_ge(a_rope, g)
                for n in (1, 0):
                    nc.scalar.activation(qks[:, n, :, :], ps[:, 2 + 2 * n:4 + 2 * n, 0:GT], ACT.Copy).then_inc(a_qks, 1)

            def attention_values(g):
                act.wait_ge(a_v, g + 1)
                if g >= 2:
                    act.wait_ge(a_pv, g - 1)
                nc.scalar.activation(vv[:, g % 2, :, :].rearrange("p (a b) d -> p a (b d)", a=2),
                                     ps[0:SEQ, 6:8, :], ACT.Copy).then_inc(a_vs, 1)

            def attention_exp(g):
                act.wait_ge(a_sub, g + 1)
                if g >= 1:
                    act.wait_ge(a_pT, g)
                nc.scalar.activation(pr[:, :, :], sc[:, :, :], ACT.Exp, scale=QSCALE).then_inc(a_exp, 1)

            def flat_high(tiles):
                for i in tiles:
                    act.wait_ge(f_tr, i + 1)
                    nc.scalar.activation(hT_n[:, 0, :, P * i:P * i + ROWS[i]],
                                         ps[:, flat_bank[i], 0:KD * P].rearrange("p (k t) -> p k t", k=KD)[:, :, 0:ROWS[i]],
                                         ACT.Copy).then_inc(f_hi, 1)

            attention_norm(0)
            attention_copy(0)
            attention_norm(1)
            attention_halves(0)
            attention_values(0)
            attention_copy(1)
            attention_norm(2)
            for g in range(NG):
                if g == NG - 1:
                    flat_high(flat_tiles_after(g - 1))
                attention_exp(g)
                if g + 1 < NG:
                    attention_halves(g + 1)
                if g + 2 < NG:
                    attention_copy(g + 2)
                if g + 1 < NG:
                    attention_values(g + 1)
                    flat_high(flat_tiles_after(g - 1))
                if g + 3 < NG:
                    attention_norm(g + 3)

            def shared_act(n0, n1):
                for n in range(n0, n1):
                    act.wait_ge(s_up, n + 1)
                    if n >= 2:
                        act.wait_ge(s_lo, n - 1)
                    nc.scalar.activation(gact[:, n % 2, :], ps[:, up_bank[n % 2], 0:SN], ACT.Gelu).then_inc(s_act, 1)

            act.wait_ge(slots_init, 32)
            def logits_copy(q):
                act.wait_ge(l_turned, q + 1)
                nc.scalar.activation(lturn[:, SN * q:SN * (q + 1)], ps[0:NE, 7, 0:SN], ACT.Copy).then_inc(l_taken, 1)

            shared_act(0, 5)
            flat_high(flat_tiles_after(NG - 1))
            logits_copy(0)
            shared_act(5, 6)
            flat_high(flat_tiles_after(NG)[:-1])
            logits_copy(1)
            flat_high(flat_tiles_after(NG)[-1:])
            shared_act(6, KF)
            logits_copy(2)
            act.wait_ge(r_sub, 1)
            nc.scalar.activation(rout[:, 1, :], rout[:, 0, :], ACT.Exp).then_inc(r_exp, 1)
            shared_act(KF, NSG * KF)

            def x_high(s, c, first=False):
                act.wait_ge(x_tr, s + 3)
                if not (first and s < 0):
                    act.wait_ge(e_up, 2 * s + 2)
                nc.scalar.activation(xgT[:, c, 0, :, :], ps[:, 4, 0:KD * P].rearrange("p (k t) -> p k t", k=KD),
                                     ACT.Copy).then_inc(x_hi, 1)

            for s in (-2, -1):
                x_high(s, s % 2, first=True)

            act.wait_ge(s_base, NT)
            i = SG * (NSG - 1)
            act.dma_start(out[P * i:P * (NT - 1), :].rearrange("(i p) d -> p i d", p=P),
                          base[:, i:NT - 1, :]).then_inc(base_out, 16)
            act.dma_start(out[P * (NT - 1):T, :], base[0:ROWS[-1], NT - 1, :]).then_inc(base_out, 16)

            def step(s, c, first=False, x=True, up=True, tr=True):
                if x:
                    x_high(s, c, first)
                if up:
                    if not (first and s < 1):
                        act.wait_ge(e_tr, 2 * s)
                    for half in range(2):
                        act.wait_ge(e_up, 2 * s + (3 + half))
                        nc.scalar.activation(hg[:, 1 - c, 512 * half:512 * (half + 1)], ps[:, hidden_bank + half, :],
                                             ACT.Gelu).then_inc(e_act, 1)
                if tr:
                    if not (first and s < 2):
                        act.wait_ge(ffn_done, s)
                    for half in range(2):
                        act.wait_ge(e_tr, 2 * s + (1 + half))
                        nc.scalar.activation(hgT[:, c, 0, 4 * half:4 * half + 4, :],
                                             ps[:, turned_bank + half, :].rearrange("p (k t) -> p k t", k=4),
                                             ACT.Copy).then_inc(e_hi, 1)

            run_steps(act, step)

        @block.tensor
        def _(te):
            def transpose(o, i, n):
                return nc.tensor.transpose(o, i, ident[0:n, 0:n])

            def ring_place(turn):
                return nc.s_assert_within(turn % 4, 0, RING - 1,
                                          skip_runtime_bounds_check_because="eplace is made of a place in the ring")

            te.wait_ge(first_in, 32)

            def tok_transposes(i):
                te.wait_ge(t_normed, i + 1)
                if i >= 2:
                    te.wait_ge(t_aff, i - 1)
                for c in range(KP):
                    last = transpose(ps[:, 2 * (i % 2) + c // 3, TOK * (c % 3):TOK * (c % 3 + 1)],
                                     xp[:, i, P * c:P * (c + 1)], TOK)
                last.then_inc(t_tr, 1)

            def tok_product(i):
                te.wait_ge(t_aff, i + 1)
                if i >= 2:
                    te.wait_ge(t_stats2, i - 1)
                for c in range(KP):
                    last = nc.tensor.matmul(ps[0:TOK, 4 + i % 2, 0:D], xT[:, i % 2, c, :], tw[:, c, :],
                                            start=c == 0, stop=c == KP - 1)
                last.then_inc(t_mm, 1)

            tok_transposes(0)
            te.wait_ge(tok_w_in, 16)
            for i in range(NTOK):
                if i + 1 < NTOK:
                    tok_transposes(i + 1)
                tok_product(i)



            def attention_transposes(g):
                te.wait_ge(a_normed, g + 1)
                if g >= 1:
                    te.wait_ge(a_low, g)
                if g >= 3:
                    te.wait_ge(a_h2, g - 2)
                for b in range(GB):
                    for c in range(KD):
                        last = transpose(ps[:, c, SEQ * b:SEQ * (b + 1)], hn[:, b, P * c:P * (c + 1)], SEQ)
                last.then_inc(a_tr, 1)

            def attention_qk(g):
                te.wait_ge(a_low, g + 1)
                if g == 0:
                    te.wait_ge(a_w, 1)
                    te.wait_ge(t_stats2, NTOK)
                else:
                    te.wait_ge(a_qks, 2 * g)
                for eo in (1, 0):
                    for w in range(2):
                        last = split_product(ps[:, 2 + 2 * eo + w, 0:GT],
                                             [([wqk2[:, v, w, c, P * eo:P * (eo + 1)] for v in range(2)],
                                               [hT[:, g % 2, v, c, :] for v in range(2)]) for c in range(KD)])
                last.then_inc(a_qk, 1)

            def attention_v(g):
                if g >= 1:
                    te.wait_ge(a_sub, g)
                    te.wait_ge(a_pTs, g)
                for b in (2, 3, 0, 1):
                    last = split_product(ps[0:SEQ, 6 + b // 2, D * (b % 2):D * (b % 2 + 1)],
                                         [([hT[:, g % 2, v, c, SEQ * b:SEQ * (b + 1)] for v in range(2)],
                                           [wv2[:, v, c, :] for v in range(2)]) for c in range(KD)])
                last.then_inc(a_v, 1)

            def attention_scores(g):
                te.wait_ge(a_rope, g + 1)
                te.wait_ge(a_vs, g + 1)
                for b in range(GB):
                    for c in range(KD):
                        last = nc.tensor.matmul(ps[0:SEQ, 7, SEQ * b:SEQ * (b + 1)], qk[:, c, 0, SEQ * b:SEQ * (b + 1)],
                                                qk[:, c, 1, SEQ * b:SEQ * (b + 1)], start=c == 0, stop=c == KD - 1)
                last.then_inc(a_scores, 1)

            def attention_probs(g):
                te.wait_ge(a_exp, g + 1)
                for b in range(GB):
                    last = transpose(ps[0:SEQ, 6, SEQ * b:SEQ * (b + 1)], pr[:, b, :], SEQ)
                last.then_inc(a_pT, 1)

            def attention_out(g):
                te.wait_ge(a_pTs, g + 1)
                te.wait_ge(a_low, min(g + 3, NG))
                for b in range(GB):
                    last = nc.tensor.matmul(ps[0:SEQ, b // 2, D * (b % 2):D * (b % 2 + 1)], prT[:, b, :],
                                            vv[:, g % 2, b, :], start=True, stop=True)
                last.then_inc(a_pv, 1)

            def flat_transposes(tiles):
                for i in tiles:
                    te.wait_ge(f_normed, i + 1)
                    if flat_bank[i] >= 2:
                        te.wait_ge(a_qks, 2 * NG)
                    if flat_bank[i] == 6:
                        te.wait_ge(a_pTs, NG)
                    if i >= 2:
                        te.wait_ge(f_lo, i - 1)
                    for c in range(KD):
                        last = transpose(ps[:, flat_bank[i], P * c:P * c + ROWS[i]],
                                         hx[0:ROWS[i], i, P * c:P * (c + 1)], ROWS[i])
                    last.then_inc(f_tr, 1)

            def x_transposes(s, c, first=False):
                te.wait_ge(x_in[c], 8 * s + (32 - 8 * c))
                if not (first and s < -1):
                    te.wait_ge(x_lo, s + 2)
                for k in range(KD):
                    last = transpose(ps[:, 4, P * k:P * (k + 1)], xg[:, c, P * k:P * (k + 1)], P)
                last.then_inc(x_tr, 1)

            def x_transposes(s, c, first=False):
                te.wait_ge(x_in[c], 8 * s + (32 - 8 * c))
                if not (first and s < -1):
                    te.wait_ge(x_lo, s + 2)
                for k in range(KD):
                    last = transpose(ps[:, 4, P * k:P * (k + 1)], xg[:, c, P * k:P * (k + 1)], P)
                last.then_inc(x_tr, 1)

            def split_product(o, pairs):
                for n, (a, b) in enumerate(pairs):
                    nc.tensor.matmul(o, a[0], b[0], start=n == 0, stop=False)
                    nc.tensor.matmul(o, a[0], b[1], start=False, stop=False)
                    last = nc.tensor.matmul(o, a[1], b[0], start=False, stop=n == len(pairs) - 1)
                return last

            def router(q):
                te.wait_ge(a_sub, NG)
                te.wait_ge(rws_ready, 1)
                te.wait_ge(f_lo, SG * (q + 1))
                if q >= 1:
                    te.wait_ge(l_taken, q)
                split_product(ps[0:NE, 7, 0:SN],
                              [([rws[:, v, c, :] for v in range(2)],
                                [hT_n[:, v, c, SN * q:SN * (q + 1)] for v in range(2)])
                               for c in range(KD)]).then_inc(l_turned, 1)

            def router_turn():
                te.wait_ge(l_taken, NSG)
                for i in range(NT):
                    last = transpose(ps[:, 7, SN + NE * i:SN + NE * (i + 1)], lturn[:, P * i:P * (i + 1)], NE)
                last.then_inc(logits, 1)

            def shared_up(n0, n1):
                for n in range(n0, n1):
                    q, f = n // KF, n % KF
                    te.wait_ge(f_lo, SG * (q + 1))
                    if n >= 2:
                        te.wait_ge(s_act, n - 1)
                    split_product(ps[:, up_bank[n % 2], 0:SN],
                                  [([ring[:, 0, v, F * c + P * f:F * c + P * (f + 1)] for v in range(2)],
                                    [hT_n[:, v, c, SN * q:SN * (q + 1)] for v in range(2)]) for c in range(KD)]
                                  ).then_inc(s_up, 1)

            def shared_down(n0, n1):
                for n in range(n0, n1):
                    q, f = n // KF, n % KF
                    te.wait_ge(s_lo, n + 1)
                    if n == 0:
                        te.wait_ge(a_h2, NG)
                    elif f == 0:
                        te.wait_ge(s_base, SG * q)
                    for j in range(SG):
                        a = [hid[:, v, f, P * j:P * (j + 1)] for v in range(2)]
                        b = [ring[:, 0, v, UPW + D * f:UPW + D * (f + 1)] for v in range(2)]
                        for m, (x, y) in enumerate(((0, 0), (0, 1), (1, 0))):
                            last = nc.tensor.matmul(ps[:, down_bank[j], 0:D], a[x], b[y], start=f == 0 and m == 0,
                                                    stop=f == KF - 1 and m == 2)
                    last.then_inc(s_down, 1)

            def shared_steps(n0, n1):
                for n in range(n0, n1):
                    shared_up(n, n + 1)
                    shared_down(n - LAG, n - LAG + 1)

            attention_transposes(0)
            attention_qk(0)
            attention_v(0)
            attention_transposes(1)
            attention_scores(0)
            for g in range(NG - 1):
                attention_qk(g + 1)
                attention_probs(g)
                if g + 2 < NG:
                    attention_transposes(g + 2)
                attention_v(g + 1)
                flat_transposes(flat_tiles_after(g - 1))
                attention_out(g)
                attention_scores(g + 1)
            flat_transposes(flat_tiles_after(NG - 2))
            attention_probs(NG - 1)
            te.wait_ge(w_ready, 4)
            te.wait_ge(f_lo, len([i for i in range(NT) if needs[i] < NG - 1]))
            shared_up(0, 2)
            attention_out(NG - 1)
            shared_up(2, 3)
            te.wait_ge(pads, 1)
            shared_steps(3, 5)
            flat_transposes(flat_tiles_after(NG - 1))
            router(0)
            shared_steps(5, 7)
            flat_transposes(flat_tiles_after(NG)[:-1])
            router(1)
            flat_transposes(flat_tiles_after(NG)[-1:])
            shared_steps(7, 8)
            router(2)
            router_turn()
            shared_steps(8, 11)
            te.wait_ge(r_mask, 1)
            te.wait_ge(f_lo, NT)
            nc.tensor.matmul(ps[:, 6, 0:NE * (NT + 1)], upper, rsel[:, :], start=True, stop=False)
            for i in range(NT):
                last = nc.tensor.matmul(ps[:, 6, NE * (i + 1):NE * (NT + 1)].rearrange("p (n e) -> p n e", e=NE), ones,
                                        rsel[:, NE * i:NE * (i + 1)].unsqueeze(1).to_broadcast([P, NT - i, NE]),
                                        start=False, stop=i == NT - 1)
            last.then_inc(r_prefix, 1)
            shared_steps(11, NSG * KF)
            te.wait_ge(r_tiles, 1)
            first_turn = te.value_load(eplace[0:1, 0:1], min_val=4, max_val=4 * NX + RING)
            for n in range(NSG * KF - LAG, NSG * KF):
                shared_down(n, n + 1)
                if n + 1 < NSG * KF:
                    x_transposes(n + 1 - NSG * KF, (n + 1 - NSG * KF) % 2, first=True)
            te.wait_ge(s_down, NSG * KF)
            te.sem_inc(ffn_done, 1)

            def step(s, c, first=False, x=True, up=True, tr=True):
                if x:
                    x_transposes(s, c, first)
                if up:
                    te.wait_ge(x_lo, s + 2)
                    if first and s == -1:
                        turn = first_turn
                    else:
                        turn = te.value_load(eplace[0:1, bass.ds(s + 1, 1)], min_val=4, max_val=4 * NX + RING)
                    te.wait_ge(w_ready, turn + 1)
                    place = ring_place(turn)
                    w = ring[:, bass.ds(place, 1), :, :].rearrange("p a v n -> p (a v) n")
                    for half in range(2):
                        if not (first and s < 0):
                            te.wait_ge(e_act, 2 * s + (1 + half))
                        split_product(ps[:, hidden_bank + half, :],
                                      [([xgT[:, 1 - c, v, k, :] for v in range(2)],
                                        [w[:, v, F * k + 512 * half:F * k + 512 * (half + 1)] for v in range(2)])
                                       for k in range(KD)]).then_inc(e_up, 1)
                if tr:
                    if first and s == 0:
                        te.wait_ge(s_base, NT)
                    for half in range(2):
                        te.wait_ge(e_act, 2 * s + (1 + half))
                        if not (first and s < 1):
                            te.wait_ge(e_lo, 2 * s + (half - 1))
                        for k in range(4):
                            f = 4 * half + k
                            last = transpose(ps[:, turned_bank + half, P * k:P * (k + 1)], hg[:, c, P * f:P * (f + 1)], P)
                        last.then_inc(e_tr, 1)
                if not (first and s < 1):
                    te.wait_ge(e_lo, 2 * s)
                    if not (first and s < 2):
                        te.wait_ge(y_ready, s - 1)
                    turn = te.value_load(eplace[0:1, bass.ds(s - 1, 1)], min_val=4, max_val=4 * NX + RING)
                    place = ring_place(turn)
                    w = ring[:, bass.ds(place, 1), :, :].rearrange("p a v n -> p (a v) n")
                    split_product(ps[:, 5, 0:D],
                                  [([hgT[:, 1 - c, v, k, :] for v in range(2)],
                                    [w[:, v, UPW + D * k:UPW + D * (k + 1)] for v in range(2)])
                                   for k in range(KF)]).then_inc(ffn_done, 1)

            run_steps(te, step)

        @block.vector
        def _(dve):
            v = nc.vector
            link_count = [0]

            def link(ins):
                link_count[0] += 1
                ins.then_inc(s_dve, 1)
                dve.wait_ge(s_dve, link_count[0])

            def tok_stats(i):
                dve.wait_ge(patches_in[i], 16)
                for j in range(2):
                    last = v.bn_stats(tst[:, i, 6 * j:6 * j + 6], xp[:, i, 384 * j:384 * (j + 1)])
                link(last)
                link(v.bn_aggr(tmv[:, i, :], tst[:, i, :]))
                v.tensor_scalar(tmv[:, i, 1:2], tmv[:, i, 1:2], EPS, None, ALU.add).then_inc(t_stats, 1)

            def tok_norm(i):
                dve.wait_ge(t_rstd, i + 1)
                v.tensor_scalar(xp[:, i, :], xp[:, i, :], tmv[:, i, 0:1], trs[:, i:i + 1], ALU.subtract,
                                ALU.mult).then_inc(t_normed, 1)

            def tok_stats2(i):
                dve.wait_ge(t_mm, i + 1)
                if i == 0:
                    dve.wait_ge(tok_vec_in, 48)
                if i >= 3:
                    dve.wait_ge(img_out[i - 3], 16)
                n = NTOK + i
                link(v.tensor_tensor(tt[:, i % 3, :], ps[0:TOK, 4 + i % 2, 0:D], vecs[:, 0, :], ALU.add))
                link(v.bn_stats(tst[:, n, 0:6], tt[:, i % 3, :]))
                link(v.bn_aggr(tmv[:, n, :], tst[:, n, 0:6]))
                v.tensor_scalar(tmv[:, n, 1:2], tmv[:, n, 1:2], EPS, None, ALU.add).then_inc(t_stats2, 1)

            def tok_norm2(i):
                dve.wait_ge(t_rstd2, i + 1)
                v.tensor_scalar(tt[:, i % 3, :], tt[:, i % 3, :], tmv[:, NTOK + i, 0:1], trs[:, NTOK + i:NTOK + i + 1],
                                ALU.subtract, ALU.mult).then_inc(t_norm2, 1)

            cos, sin = (rope[:, n:n + 1, :].to_broadcast([P, 2 * GB, SEQ]) for n in range(2))

            def attention_front(g):
                dve.wait_ge(h_in[g], 16)
                if g == 0:
                    dve.wait_ge(text_in, 32)
                for b in range(GB):
                    last = v.bn_stats(ast[:, g, b, :], h[:, GB * g + b, :])
                link(last)
                for b in range(GB):
                    last = v.bn_aggr(amv[:, g, b, :], ast[:, g, b, :])
                link(last)
                v.tensor_scalar(amv[:, g, :, 1], amv[:, g, :, 1], EPS, None, ALU.add).then_inc(a_stats, 1)

            def attention_bias(g):
                dve.wait_ge(a_rstd, g + 1)
                v.scalar_tensor_tensor(out=anb[:, g, :], in0=amv[:, g, :, 0], scalar=-1.0, in1=ars[:, g, :],
                                       op0=ALU.mult, op1=ALU.mult).then_inc(a_norm_in, 1)

            def attention_low(g):
                dve.wait_ge(a_hT, g + 1)
                v.tensor_tensor(hT[:, g % 2, 1, :, :], ps[:, 0:2, 0:GT], hT[:, g % 2, 0, :, :].bitcast(F32),
                                ALU.subtract).then_inc(a_low, 1)

            def attention_weights():
                dve.wait_ge(attn_w_in, 48)
                v.tensor_copy(wqk2[:, 0, :, :, :], wqk[:, :, :, :])
                link(v.tensor_copy(wv2[:, 0, :, :], wvs[:, :, :]))
                v.tensor_tensor(wqk2[:, 1, :, :, :], wqk[:, :, :, :], wqk2[:, 0, :, :, :].bitcast(F32), ALU.subtract)
                v.tensor_tensor(wv2[:, 1, :, :], wvs[:, :, :], wv2[:, 0, :, :].bitcast(F32),
                                ALU.subtract).then_inc(a_w, 1)

            def attention_rope(g):
                if g == 0:
                    dve.wait_ge(rope_in, 16)
                else:
                    dve.wait_ge(a_scores, g)
                wide = lambda x: x.rearrange("p w (b s) -> p (w b) s", b=GB)
                for n in (1, 0):
                    dve.wait_ge(a_qks, 2 * g + 2 - n)
                    last = v.tensor_tensor(wide(qk[:, n, :, :]), wide(qks[:, n, :, :]), cos, ALU.mult)
                if g == 0:
                    last = v.tensor_tensor(wide(qsin[:, 0, :, :]), wide(qks[:, 0, :, :]), sin, ALU.mult)
                link(last)
                if 1 <= g < NG - 1:
                    attention_low(g + 1)
                if g == NG - 1:
                    for i in flat_tiles_after(g - 1):
                        flat_stats(i)
                dve.wait_ge(a_sin, 2 * g + 1)
                link(v.tensor_tensor(qk[:, 0, :, :], qk[:, 0, :, :], qsin[:, 1, :, :], ALU.add))
                dve.wait_ge(a_sin, 2 * g + 2)
                v.tensor_tensor(qk[:, 1, :, :], qk[:, 1, :, :], qsin[:, 0, :, :], ALU.subtract).then_inc(a_rope, 1)

            def attention_softmax(g):
                dve.wait_ge(a_scores, g + 1)
                s3 = ps[0:SEQ, 7, 0:GT].rearrange("p (b s) -> p b s", b=GB)
                link(v.tensor_reduce(asm[:, 0, :], s3, AX.X, ALU.max))
                if g >= 1:
                    dve.wait_ge(a_exp, g)
                v.tensor_tensor(sc[:, :, :], s3, asm[:, 0, :].unsqueeze(2).to_broadcast([SEQ, GB, SEQ]),
                                ALU.subtract).then_inc(a_sub, 1)

            def attention_sums(g):
                dve.wait_ge(a_exp, g + 1)
                link(v.tensor_reduce(asm[:, 1, :], pr[:, :, :], AX.X, ALU.add))
                link(v.reciprocal(asm[:, 2, :], asm[:, 1, :]))

            def attention_probs(g):
                dve.wait_ge(a_pT, g + 1)
                if g >= 1:
                    dve.wait_ge(a_pv, g)
                v.tensor_copy(prT[:, :, :], ps[0:SEQ, 6, 0:GT].rearrange("p (b s) -> p b s", b=GB)).then_inc(a_pTs, 1)

            def attention_end(g):
                dve.wait_ge(a_pv, g + 1)
                for b in range(GB):
                    last = v.scalar_tensor_tensor(
                        out=h[:, GB * g + b, :], in0=ps[0:SEQ, b // 2, D * (b % 2):D * (b % 2 + 1)],
                        scalar=asm[:, 2, b:b + 1], in1=h[:, GB * g + b, :], op0=ALU.mult, op1=ALU.add)
                last.then_inc(a_h2, 1)

            def flat_stats(i):
                r = ROWS[i]
                dve.wait_ge(f_in[i % NBUF_FLAT], 16 * (i // NBUF_FLAT + 1))
                link(v.bn_stats(st2[0:r, i, :], h2f[0:r, i % NBUF_FLAT, :]))
                link(v.bn_aggr(mv2[0:r, i, :], st2[0:r, i, :]))
                v.tensor_scalar(mv2[0:r, i, 1:2], mv2[0:r, i, 1:2], EPS, None, ALU.add).then_inc(f_stats, 1)

            def flat_norm(i):
                r = ROWS[i]
                dve.wait_ge(f_rstd, i + 1)
                v.tensor_scalar(hx[0:r, i, 0:D], h2f[0:r, i % NBUF_FLAT, :], mv2[0:r, i, 0:1], rs2[0:r, i:i + 1], ALU.subtract,
                                ALU.mult).then_inc(f_normed, 1)

            def flat_low(tiles):
                for i in tiles:
                    r = ROWS[i]
                    dve.wait_ge(f_hi, i + 1)
                    cols = slice(P * i, P * i + r)
                    v.tensor_tensor(hT_n[:, 1, :, cols],
                                    ps[:, flat_bank[i], 0:KD * P].rearrange("p (k t) -> p k t", k=KD)[:, :, 0:r],
                                    hT_n[:, 0, :, cols].bitcast(F32), ALU.subtract).then_inc(f_lo, 1)

            for k in range(NTOK + 4):
                if k < NTOK:
                    tok_stats(k)
                if 0 <= k - 1 < NTOK:
                    tok_norm(k - 1)
                if k == NTOK + 3:
                    attention_low(0)
                if 0 <= k - 4 < NTOK:
                    tok_norm2(k - 4)
                if k == NTOK + 1:
                    attention_front(0)
                if 0 <= k - 3 < NTOK:
                    tok_stats2(k - 3)
                if k == NTOK + 1:
                    attention_bias(0)
                    attention_weights()

            attention_front(1)
            attention_bias(1)
            dve.wait_ge(consts_in, 16)
            link(v.memset(gact[:, 0, 0:XW], 0.0))
            v.memset(gact[:, 0, C_EXP:C_EXP + 2], -1.0)
            v.tensor_copy(gact[:, 0, C_TOK:C_TOK + 1], small[:, S_TOK + NT:S_TOK + NT + 1]).then_inc(empty_row, 1)
            v.tensor_copy(hx[:, :, C_TOK], small[:, S_TOK:S_TOK + NT])
            dve.wait_ge(router_in, 16)
            link(v.tensor_copy(rws[:, 0, :, :], rw[:, :, :]))
            v.tensor_tensor(rws[:, 1, :, :], rw[:, :, :], rws[:, 0, :, :].bitcast(F32), ALU.subtract).then_inc(rws_ready, 1)

            def shared_parts(n0, n1):
                for n in range(n0, n1):
                    q, f = n // KF, n % KF
                    dve.wait_ge(s_act, n + 1)
                    if q >= 1:
                        dve.wait_ge(s_down, n - KF + 1)
                    link(v.tensor_copy(hid[:, 0, f, :], gact[:, n % 2, :]))
                    v.tensor_tensor(hid[:, 1, f, :], gact[:, n % 2, :], hid[:, 0, f, :].bitcast(F32),
                                    ALU.subtract).then_inc(s_lo, 1)

            def shared_end(i0, i1):
                for i in range(i0, i1):
                    dve.wait_ge(s_down, KF * (i // SG + 1))
                    dve.wait_ge(f_base, i + 1)
                    r = ROWS[i]
                    v.tensor_tensor(base[0:r, i, :], base[0:r, i, :], ps[0:r, down_bank[i % SG], 0:D], ALU.add).then_inc(s_base, 1)

            attention_front(2)
            attention_rope(0)
            attention_low(1)
            attention_bias(2)
            for g in range(NG - 1):
                attention_softmax(g)
                for i in flat_tiles_after(g - 1):
                    flat_norm(i)
                if g == 0:
                    attention_front(3)
                attention_sums(g)
                attention_probs(g)
                attention_rope(g + 1)
                if g == 0:
                    attention_bias(3)
                for i in flat_tiles_after(g):
                    if g < NG - 2:
                        flat_stats(i)
                    else:
                        flat_norm(i)
                flat_low(flat_tiles_after(g - 1))
                if g < NG - 2:
                    attention_end(g)

            g = NG - 1
            attention_softmax(g)
            flat_low(flat_tiles_after(g - 1))
            attention_end(g - 1)
            attention_sums(g)
            attention_probs(g)
            dve.wait_ge(slots_init, 32)
            shared_parts(0, 1)
            attention_end(g)
            shared_parts(1, 2)
            for i in flat_tiles_after(g):
                flat_stats(i)
            for i in flat_tiles_after(NG - 1):
                flat_norm(i)
            shared_parts(2, 3)
            flat_low(flat_tiles_after(NG - 1))
            shared_parts(3, 4)
            for i in flat_tiles_after(NG):
                flat_stats(i)
            for i in flat_tiles_after(NG):
                flat_norm(i)
            shared_parts(4, 5)
            flat_low(flat_tiles_after(NG))
            shared_parts(5, KF)

            n3 = lambda a: a.rearrange("p (n e) -> p n e", e=NE)
            over_e = lambda a: a.unsqueeze(2).to_broadcast([P, NT, NE])
            rank = small[:, S_RANK:S_RANK + NE].unsqueeze(1).to_broadcast([P, NT, NE])
            dve.wait_ge(logits, 1)
            lg = n3(ps[:, 7, SN:SN + NT * NE])
            link(v.tensor_reduce(rsm[:, 0, :], lg, AX.X, ALU.max))
            v.tensor_tensor(n3(rout[:, 0, :]), lg, over_e(rsm[:, 0, :]), ALU.subtract).then_inc(r_sub, 1)
            dve.wait_ge(r_exp, 1)
            link(v.tensor_reduce(rsm[:, 1, :], n3(rout[:, 1, :]), AX.X, ALU.add))
            link(v.reciprocal(rsm[:, 2, :], rsm[:, 1, :]))
            link(v.tensor_tensor(n3(rout[:, 2, :]), n3(rout[:, 1, :]), over_e(rsm[:, 2, :]), ALU.mult))
            for k in range(2):
                pk, gk = rout[:, 2 + k, :], rsm[:, 3 + k, :]
                pick = rpick[:, k, :]
                link(v.tensor_reduce(gk, n3(pk), AX.X, ALU.max))
                link(v.tensor_tensor(n3(rout[:, 4, :]), n3(pk), over_e(gk), ALU.is_equal))
                link(v.tensor_tensor(n3(rout[:, 4, :]), n3(rout[:, 4, :]), rank, ALU.mult))
                link(v.tensor_reduce(rsm[:, 5 + k, :], n3(rout[:, 4, :]), AX.X, ALU.max))
                link(v.tensor_tensor(n3(pick), over_e(rsm[:, 5 + k, :]), rank, ALU.is_equal))
                if k == 0:
                    link(v.scalar_tensor_tensor(out=rout[:, 3, :], in0=pick, scalar=-2.0, in1=pk,
                                                op0=ALU.mult, op1=ALU.add))
            link(v.tensor_tensor(rsel[:, 0:NE * NT], rpick[:, 0, :], rpick[:, 1, :], ALU.add))
            v.memset(rsel[:, NE * NT:], 0.0)
            link(v.tensor_tensor(n3(rsel[:, 0:NE * NT]), n3(rsel[:, 0:NE * NT]),
                                 over_e(small[:, S_VALID:S_VALID + NT]), ALU.mult))
            for k in range(2):
                v.tensor_copy(hx[:, :, C_GATE + k], rsm[:, 3 + k, :])
                last = v.tensor_scalar(hx[:, :, C_EXP + k], rsm[:, 5 + k, :], -1.0, float(NE), ALU.mult, ALU.add)
            last.then_inc(r_mask, 1)

            shared_parts(KF, KF + 1)
            shared_end(0, SG)
            shared_parts(KF + 1, KF + 2)

            dve.wait_ge(r_prefix, 1)
            link(v.tensor_copy(rtab[:, 0, :], ps[:, 6, NE * NT:NE * (NT + 1)]))
            c3 = rcmp[:, :].rearrange("p (e k) -> p e k", k=CAP)
            link(v.tensor_tensor(c3, rtab[:, 0, :].unsqueeze(2).to_broadcast([P, NE, CAP]),
                                 small[:, S_THR:S_THR + CAP].unsqueeze(1).to_broadcast([P, NE, CAP]), ALU.is_gt))
            link(v.tensor_reduce(rtab[:, 1, :], c3, AX.X, ALU.add))
            link(v.tensor_tensor_scan(rtab[:, 2, :], small[:, S_ONE:S_ONE + NE], rtab[:, 1, :], 0.0, ALU.mult, ALU.add))
            link(v.tensor_tensor(rtab[:, 3, :], rtab[:, 2, :], rtab[:, 1, :], ALU.subtract))
            link(v.tensor_scalar(rtab[:, 3, :], rtab[:, 3, :], float(P), None, ALU.mult))
            link(v.tensor_tensor(n3(rout[:, 5, :]), n3(ps[:, 6, 0:NE * NT]),
                                 rtab[:, 3, :].unsqueeze(1).to_broadcast([P, NT, NE]), ALU.add))
            for k in range(2):
                link(v.tensor_tensor(rout[:, 6 + k, :], rout[:, 5, :], rpick[:, k, :], ALU.mult))
                link(v.tensor_reduce(rsm[:, k, :], n3(rout[:, 6 + k, :]), AX.X, ALU.add))
                link(v.tensor_copy(slot_i[:, k, :], rsm[:, k, :]))
            v.tensor_copy(tend_int[:, :], rtab[0:1, 2, :]).then_inc(r_slots, 1)
            shared_parts(KF + 2, KF + 4)
            e3 = ecmp[:, :].rearrange("p (t e) -> p t e", e=NE)
            link(v.tensor_tensor(e3, small[:, S_TILE:S_TILE + TILES].unsqueeze(2).to_broadcast([P, TILES, NE]),
                                 rtab[:, 2, :].unsqueeze(1).to_broadcast([P, TILES, NE]), ALU.is_ge))
            link(v.tensor_reduce(etab[:, :], e3, AX.X, ALU.add))
            link(v.tensor_scalar(etab[:, :], etab[:, :], float(NE - 1), None, ALU.min))
            link(v.tensor_scalar(ekeep[:, 0, :], etab[0:1, :], float(RING - 1), float(-RING), ALU.is_ge, ALU.mult))
            link(v.tensor_scalar(ekeep[:, 1, :], etab[0:1, :], float(2 * RING - 1), float(-RING), ALU.is_ge, ALU.mult))
            link(v.tensor_tensor(ekeep[:, 0, :], ekeep[:, 0, :], ekeep[:, 1, :], ALU.add))
            link(v.tensor_scalar(ekeep[:, 1, :], etab[0:1, :], 5.0, 5.0, ALU.mult, ALU.add))
            v.tensor_tensor(eplace[:, :], ekeep[:, 0, :], ekeep[:, 1, :], ALU.add).then_inc(r_tiles, 1)

            shared_parts(KF + 4, 2 * KF + 2)
            shared_end(SG, 2 * SG)
            def x_low(s, c, first=False):
                dve.wait_ge(x_in[c], 8 * s + (32 - 8 * c))
                et = etab[:, bass.ds(s + 2, 1)]
                if not (first and s < 0):
                    dve.wait_ge(x_meta, s + 1)
                v.scalar_tensor_tensor(out=junk[:, c, :], in0=xg[:, c, C_EXP:C_EXP + 2], scalar=et,
                                       in1=xg[:, c, C_GATE:C_GATE + 2], op0=ALU.is_equal, op1=ALU.mult,
                                       accum_out=gate[:, bass.ds(s + 2, 1)])
                v.tensor_copy(dest[:, bass.ds(s + 2, 1)], xg[:, c, C_TOK:C_TOK + 1]).then_inc(x_meta, 1)
                dve.wait_ge(x_hi, s + 3)
                v.tensor_tensor(xgT[:, c, 1, :, :], ps[:, 4, 0:KD * P].rearrange("p (k t) -> p k t", k=KD),
                                xgT[:, c, 0, :, :].bitcast(F32), ALU.subtract).then_inc(x_lo, 1)

            shared_parts(2 * KF + 2, 3 * KF)
            for s in (-2, -1):
                x_low(s, s % 2, first=True)
            shared_end(2 * SG, NT)

            tile_no = small[0:1, S_TILE:S_TILE + TILES]
            link(v.tensor_tensor(e3[0:1], e3[0:1], rtab[0:1, 2, :].unsqueeze(1).to_broadcast([1, TILES, NE]), ALU.mult))
            link(v.tensor_reduce(ytab[:, 0, :], e3[0:1], AX.X, ALU.max))
            link(v.scalar_tensor_tensor(out=ytab[:, 1, :], in0=tile_no, scalar=rtab[0:1, 2, NE - 1:NE], in1=tile_no,
                                        op0=ALU.is_ge, op1=ALU.mult))
            link(v.tensor_tensor(ytab[:, 0, :], ytab[:, 0, :], ytab[:, 1, :], ALU.max))
            v.tensor_scalar(additions[:, :], ytab[:, 0, :], 1.0, 16.0, ALU.max, ALU.mult).then_inc(r_additions, 1)

            def step(s, c, first=False, x=True, up=True, tr=True):
                if x:
                    x_low(s, c, first)
                if tr:
                    for half in range(2):
                        dve.wait_ge(e_hi, 2 * s + (1 + half))
                        v.tensor_tensor(hgT[:, c, 1, 4 * half:4 * half + 4, :],
                                        ps[:, turned_bank + half, :].rearrange("p (k t) -> p k t", k=4),
                                        hgT[:, c, 0, 4 * half:4 * half + 4, :].bitcast(F32),
                                        ALU.subtract).then_inc(e_lo, 1)
                if not (first and s < 1):
                    dve.wait_ge(ffn_done, s + 1)
                    dve.wait_ge(x_meta, s)
                    v.tensor_scalar(y_all[:, bass.ds(s - 1, 1), :].rearrange("p a d -> p (a d)"), ps[:, 5, 0:D],
                                    gate[:, bass.ds(s - 1, 1)], None, ALU.mult).then_inc(y_ready, 1)

            run_steps(dve, step)


def kernel(**inputs):
    import numpy as np
    import concourse.bacc as bacc
    from concourse.bass_utils import run_bass_kernel_spmd

    a = {k.removeprefix("L0_"): np.asarray(v) for k, v in inputs.items()}
    f32 = np.float32
    side, ps = 6, 16

    patches = a["x"].reshape(NB, 3, side, ps, side, ps).transpose(0, 2, 4, 3, 5, 1).reshape(NB * NPATCH, PATCH)
    halves = np.concatenate([np.arange(0, D, 2), np.arange(1, D, 2)])
    up = np.concatenate([a["ffn_shared_up"], a["ffn_routed_up"]])
    down = np.concatenate([a["ffn_shared_down"], a["ffn_routed_down"]])

    k = np.arange(P)
    mats = np.stack([np.eye(P), k[:, None] < k[None, :], np.ones((P, P))], 1).astype(f32)
    tok = P * np.arange(NT + 1)[None, :] + k[:, None]
    tok[:, NT] = T + k
    row = lambda x: np.broadcast_to(np.asarray(x)[None, :], (P, len(x)))
    small = np.concatenate([tok[:, :NT] < T, row(NE - np.arange(NE)), row(np.r_[-1, P * np.arange(1, CAP)]), row(np.arange(TILES)),
                            tok, row(np.ones(NE))], 1).astype(f32)
    omega = (1.0 / f32(10000.0) ** (np.arange(D // 4, dtype=f32) / f32(D // 4 - 1))).astype(f32)
    yy, xx = np.meshgrid(np.arange(side), np.arange(side), indexing="ij")
    ya, xa = (v.reshape(-1)[:, None].astype(f32) * omega[None, :] for v in (yy, xx))
    pe = np.concatenate([np.sin(xa), np.cos(xa), np.sin(ya), np.cos(ya)], 1).astype(f32)
    pe = pe[np.arange(NB * NPATCH) % NPATCH].reshape(NTOK, TOK, D).transpose(1, 0, 2)
    theta = np.power(f32(10000.0), (f32(-2.0) * (np.arange(D // 2, dtype=f32) - f32(1.0)) / f32(D)).astype(f32)).astype(f32)
    angle = theta[:, None] * np.arange(SEQ, dtype=f32)[None, :]
    rope = np.stack([np.cos(angle), np.sin(angle)], 1).astype(f32)

    arrays = {
        "patches": patches, "txt": a["txt"], "cls_token": a["tok_cls_token"].reshape(1, D),
        "cls_pos": a["tok_cls_pos_embedding"].reshape(1, D), "ln1_gb": np.stack([a["tok_ln1_g"], a["tok_ln1_b"]]).reshape(2, KP, P).transpose(2, 0, 1),
        "tok_w": a["tok_W"], "tok_bias": a["tok_bias"], "ln2_g": a["tok_ln2_g"], "ln2_b": a["tok_ln2_b"],
        "wq": a["attn_wq"][halves].T, "wk": a["attn_wk"][halves].T, "wv": a["attn_wv"].T,
        "w_up": up.reshape(NX, KD, P, F).transpose(0, 2, 1, 3).reshape(NX, P, UPW),
        "w_dn": down.reshape(NX, KF, P, D).transpose(0, 2, 1, 3).reshape(NX, P, UPW),
        "router_w": a["ffn_router_w"], "c_mats": mats, "c_small": small, "c_pe": pe, "c_rope": rope,
    }
    nc = bacc.Bacc("TRN2", target_bir_lowering=False, num_devices=1)
    data, args = {}, {}
    for name, v in arrays.items():
        data[f"in_{name}"] = np.ascontiguousarray(v)
        args[name] = nc.dram_tensor(f"in_{name}", v.shape, F32, kind="ExternalInput").ap()
    args["out"] = nc.dram_tensor("out_tokens", (T + P, D), F32, kind="ExternalOutput").ap()
    fusion_layer(nc, **args)
    r = run_bass_kernel_spmd(nc, [data], core_ids=[0])
    return r.results[0]["out_tokens"][:T].reshape(NB, SEQ, D)
```
